# Optimizing a Trainium2 kernel written in Bass

```python
import numpy as np
import jax
import jax.numpy as jnp

def _softmax(x, axis=-1):
    return jax.nn.softmax(x, axis=axis)

def _gelu(x):
    return jax.nn.gelu(x, approximate=True)

def _silu(x):
    return jax.nn.silu(x)

def _sigmoid(x):
    return jax.nn.sigmoid(x)

def _layernorm(x, axis=-1, eps=1e-05):
    m = jnp.mean(x, axis=axis, keepdims=True)
    v = jnp.var(x, axis=axis, keepdims=True)
    return (x - m) / jnp.sqrt(v + eps)

def _scatter_add(tgt, idx, src, axis=0):
    return tgt.at[idx].add(src)

def _segment_sum(src, seg, n):
    return jax.ops.segment_sum(src, seg, n)
kernel_name = 'mk_adj_resnorm_d4_adj_r2_5c4e47'

def setup_inputs(seed: int=0):
    np.random.seed(seed)
    _w = jnp.asarray

    def _rec_inputs():
        import jax
        import jax.numpy as jnp
        _gk = jax.random.key(seed)
        x = -0.0001538 + 1 * jax.random.normal(jax.random.fold_in(_gk, 1), (32, 256, 384), jnp.float32)
        _a = jax.random.bernoulli(jax.random.fold_in(_gk, 2), 0.0625, (32, 256, 256))
        _af = _a.astype(jnp.float32)
        _af = _af * jax.random.uniform(jax.random.fold_in(_gk, 3), (32, 256, 256), jnp.float32, 0.05, 0.999992)
        adj = _af
        return (x, adj)
    x, adj = _rec_inputs()

    def _L0_gnn_setup():
        import jax, jax.numpy as jnp
        import numpy as np
        B, N, D, H = (8, 512, 384, 12)
        HD = D // H

        def _split_heads(x):
            b, n, _ = x.shape
            return x.reshape(b, n, H, HD).transpose(0, 2, 1, 3)
        key = jax.random.key(seed)
        ks = jax.random.split(key, 10)
        input_graph = jax.random.normal(ks[0], (B, N, D), dtype=jnp.float32)
        u = jax.random.uniform(ks[1], (B, N, N), dtype=jnp.float32)
        keep = jax.random.uniform(ks[2], (B, N, N)) < 0.15
        adj = jnp.where(keep, u, 0.0)
        s = 1.0 / np.sqrt(D)
        Wq = jax.random.normal(ks[3], (D, D), dtype=jnp.float32) * s
        bq = jnp.zeros((D,), dtype=jnp.float32)
        Wk = jax.random.normal(ks[4], (D, D), dtype=jnp.float32) * s
        bk = jnp.zeros((D,), dtype=jnp.float32)
        Wv = jax.random.normal(ks[5], (D, D), dtype=jnp.float32) * s
        bv = jnp.zeros((D,), dtype=jnp.float32)
        beta = jnp.asarray(0.1, dtype=jnp.float32)
        return {'input_graph': input_graph, 'adj': adj, 'Wq': Wq, 'bq': bq, 'Wk': Wk, 'bk': bk, 'Wv': Wv, 'bv': bv, 'beta': beta}
    _L0_gnn_all = _L0_gnn_setup()
    _L0_gnn_in = {k: v for k, v in _L0_gnn_all.items() if k in ('Wq', 'bq', 'Wk', 'bk', 'Wv', 'bv', 'beta')}
    del _L0_gnn_all

    def _L1_gnn_setup():
        import jax, jax.numpy as jnp
        import numpy as np
        NUM_HEADS = 12
        HIDDEN = 384
        HEAD = HIDDEN // NUM_HEADS
        SCALE = HIDDEN ** (-0.5)
        key = jax.random.key(seed)
        ks = jax.random.split(key, 8)
        B, N = (16, 256)
        std = HIDDEN ** (-0.5)
        return {'x': jax.random.normal(ks[0], (B, N, HIDDEN), dtype=jnp.float32), 'encoding_bias': jax.random.normal(ks[1], (B, N, N), dtype=jnp.float32), 'Wq': jax.random.normal(ks[2], (HIDDEN, HIDDEN), dtype=jnp.float32) * std, 'Wk': jax.random.normal(ks[3], (HIDDEN, HIDDEN), dtype=jnp.float32) * std, 'Wv': jax.random.normal(ks[4], (HIDDEN, HIDDEN), dtype=jnp.float32) * std, 'bv': jax.random.normal(ks[5], (HIDDEN,), dtype=jnp.float32) * 0.01, 'Wo': jax.random.normal(ks[6], (HIDDEN, HIDDEN), dtype=jnp.float32) * std, 'bo': jax.random.normal(ks[7], (HIDDEN,), dtype=jnp.float32) * 0.01}
    _L1_gnn_all = _L1_gnn_setup()
    _L1_gnn_in = {k: v for k, v in _L1_gnn_all.items() if k in ('Wq', 'Wk', 'Wv', 'bv', 'Wo', 'bo')}
    del _L1_gnn_all

    def _L2_gnn_setup():
        import jax, jax.numpy as jnp
        import numpy as np
        LN_EPS = 1e-12

        def _digcn_forward(hidden_state, adjacency_matrix, Wl, bl, Ws, bs, Wr, br, ln_w, ln_b):
            B, S, D = hidden_state.shape
            temper = jnp.asarray(D, jnp.float32) ** 0.5
            i = jnp.arange(S)
            upper = (i[None, :] > i[:, None]).astype(hidden_state.dtype)
            lower = (i[None, :] < i[:, None]).astype(hidden_state.dtype)

            def layer(h, params):
                wl, b_l, ws, b_s, wr, b_r, g, beta = params
                u = jnp.einsum('bid,bjd->bij', h, h) / temper
                a = jax.nn.softmax(u, axis=-1)
                delta = a * adjacency_matrix
                attn = delta / (jnp.sum(delta, axis=-1, keepdims=True) + 1e-10)
                hl = h @ wl.T + b_l
                hs = h @ ws.T + b_s
                hr = h @ wr.T + b_r
                diag_a = jnp.diagonal(attn, axis1=1, axis2=2)
                ctx = jnp.einsum('bij,bjd->bid', attn * upper, hl) + diag_a[..., None] * hs + jnp.einsum('bij,bjd->bid', attn * lower, hr)
                mean = ctx.mean(-1, keepdims=True)
                var = ctx.var(-1, keepdims=True)
                o = (ctx - mean) / jnp.sqrt(var + LN_EPS) * g + beta
                return (jax.nn.relu(o), None)
            out, _ = jax.lax.scan(layer, hidden_state, (Wl, bl, Ws, bs, Wr, br, ln_w, ln_b))
            return out
        key = jax.random.key(seed)
        ks = jax.random.split(key, 6)
        B, S, D, L = (8, 512, 384, 2)
        scale = (1.0 / D) ** 0.5
        hidden_state = jax.random.normal(ks[0], (B, S, D), jnp.float32)
        adjacency_matrix = (jax.random.uniform(ks[1], (B, S, S)) < 0.05).astype(jnp.float32)
        Wl = jax.random.normal(ks[2], (L, D, D), jnp.float32) * scale
        Ws = jax.random.normal(ks[3], (L, D, D), jnp.float32) * scale
        Wr = jax.random.normal(ks[4], (L, D, D), jnp.float32) * scale
        bl = jnp.zeros((L, D), jnp.float32)
        bs = jnp.zeros((L, D), jnp.float32)
        br = jnp.zeros((L, D), jnp.float32)
        ln_w = jnp.ones((L, D), jnp.float32)
        ln_b = jnp.zeros((L, D), jnp.float32)
        return dict(hidden_state=hidden_state, adjacency_matrix=adjacency_matrix, Wl=Wl, bl=bl, Ws=Ws, bs=bs, Wr=Wr, br=br, ln_w=ln_w, ln_b=ln_b)
    _L2_gnn_all = _L2_gnn_setup()
    _L2_gnn_in = {k: v for k, v in _L2_gnn_all.items() if k in ('Wl', 'bl', 'Ws', 'bs', 'Wr', 'br', 'ln_w', 'ln_b')}
    del _L2_gnn_all

    def _L3_gnn_setup():
        import jax, jax.numpy as jnp
        import numpy as np
        NUM_HEADS = 12
        HIDDEN = 384
        HEAD = HIDDEN // NUM_HEADS
        B, N = (16, 256)
        key = jax.random.key(seed)
        ks = jax.random.split(key, 9)
        s = 0.02
        return {'x': jax.random.normal(ks[0], (B, N, HIDDEN), jnp.float32), 'spatial_encoding': jax.random.normal(ks[1], (B, N, N), jnp.float32), 'edge_encoding': jax.random.normal(ks[2], (B, N, N), jnp.float32), 'Wq': jax.random.normal(ks[3], (HIDDEN, HIDDEN), jnp.float32) * s, 'Wk': jax.random.normal(ks[4], (HIDDEN, HIDDEN), jnp.float32) * s, 'Wv': jax.random.normal(ks[5], (HIDDEN, HIDDEN), jnp.float32) * s, 'bv': jax.random.normal(ks[6], (HIDDEN,), jnp.float32) * s, 'Wo': jax.random.normal(ks[7], (HIDDEN, HIDDEN), jnp.float32) * s, 'bo': jax.random.normal(ks[8], (HIDDEN,), jnp.float32) * s}
    _L3_gnn_all = _L3_gnn_setup()
    _L3_gnn_in = {k: v for k, v in _L3_gnn_all.items() if k in ('Wq', 'Wk', 'Wv', 'bv', 'Wo', 'bo')}
    del _L3_gnn_all
    return {'x': x, 'adj': adj, 'L0_gnn_Wq': _L0_gnn_in['Wq'], 'L0_gnn_bq': _L0_gnn_in['bq'], 'L0_gnn_Wk': _L0_gnn_in['Wk'], 'L0_gnn_bk': _L0_gnn_in['bk'], 'L0_gnn_Wv': _L0_gnn_in['Wv'], 'L0_gnn_bv': _L0_gnn_in['bv'], 'L0_gnn_beta': _L0_gnn_in['beta'], 'L1_gnn_Wq': _L1_gnn_in['Wq'], 'L1_gnn_Wk': _L1_gnn_in['Wk'], 'L1_gnn_Wv': _L1_gnn_in['Wv'], 'L1_gnn_bv': _L1_gnn_in['bv'], 'L1_gnn_Wo': _L1_gnn_in['Wo'], 'L1_gnn_bo': _L1_gnn_in['bo'], 'L2_gnn_Wl': _L2_gnn_in['Wl'], 'L2_gnn_bl': _L2_gnn_in['bl'], 'L2_gnn_Ws': _L2_gnn_in['Ws'], 'L2_gnn_bs': _L2_gnn_in['bs'], 'L2_gnn_Wr': _L2_gnn_in['Wr'], 'L2_gnn_br': _L2_gnn_in['br'], 'L2_gnn_ln_w': _L2_gnn_in['ln_w'], 'L2_gnn_ln_b': _L2_gnn_in['ln_b'], 'L3_gnn_Wq': _L3_gnn_in['Wq'], 'L3_gnn_Wk': _L3_gnn_in['Wk'], 'L3_gnn_Wv': _L3_gnn_in['Wv'], 'L3_gnn_bv': _L3_gnn_in['bv'], 'L3_gnn_Wo': _L3_gnn_in['Wo'], 'L3_gnn_bo': _L3_gnn_in['bo']}

def reference(x, adj, L0_gnn_Wq, L0_gnn_bq, L0_gnn_Wk, L0_gnn_bk, L0_gnn_Wv, L0_gnn_bv, L0_gnn_beta, L1_gnn_Wq, L1_gnn_Wk, L1_gnn_Wv, L1_gnn_bv, L1_gnn_Wo, L1_gnn_bo, L2_gnn_Wl, L2_gnn_bl, L2_gnn_Ws, L2_gnn_bs, L2_gnn_Wr, L2_gnn_br, L2_gnn_ln_w, L2_gnn_ln_b, L3_gnn_Wq, L3_gnn_Wk, L3_gnn_Wv, L3_gnn_bv, L3_gnn_Wo, L3_gnn_bo):
    import jax
    import jax.numpy as jnp

    def _L0_gnn_ref(input_graph, adj, Wq, bq, Wk, bk, Wv, bv, beta):
        import jax, jax.numpy as jnp
        import numpy as np
        B, N, D, H = (8, 512, 384, 12)
        HD = D // H

        def _split_heads(x):
            b, n, _ = x.shape
            return x.reshape(b, n, H, HD).transpose(0, 2, 1, 3)
        q = _split_heads(input_graph @ Wq + bq)
        k = _split_heads(input_graph @ Wk + bk)
        v = _split_heads(input_graph @ Wv + bv)
        scores = jnp.einsum('bhqd,bhkd->bhqk', q, k) / jnp.sqrt(jnp.asarray(HD, input_graph.dtype))
        adj_e = adj[:, None, :, :]
        scores = scores + beta * adj_e
        scores = jnp.where(adj_e > 0, scores, jnp.asarray(-9000000000000000.0, scores.dtype))
        probs = jax.nn.softmax(scores, axis=-1)
        out = jnp.einsum('bhqk,bhkd->bhqd', probs, v)
        return out.transpose(0, 2, 1, 3).reshape(input_graph.shape[0], input_graph.shape[1], D)

    def _L1_gnn_ref(x, encoding_bias, Wq, Wk, Wv, bv, Wo, bo):
        import jax, jax.numpy as jnp
        import numpy as np
        NUM_HEADS = 12
        HIDDEN = 384
        HEAD = HIDDEN // NUM_HEADS
        SCALE = HIDDEN ** (-0.5)
        B, N, _ = x.shape
        q = (x @ Wq.T).reshape(B, N, NUM_HEADS, HEAD)
        k = (x @ Wk.T).reshape(B, N, NUM_HEADS, HEAD)
        v = (x @ Wv.T + bv).reshape(B, N, NUM_HEADS, HEAD)
        a = jnp.einsum('bnhd,bmhd->bhnm', q, k) * SCALE + encoding_bias[:, None, :, :]
        pad_mask = jnp.all(a == 0, axis=-1)
        a = jnp.where(pad_mask[..., None], -jnp.inf, a)
        a = jax.nn.softmax(a, axis=-1)
        a = jnp.nan_to_num(a)
        o = jnp.einsum('bhnm,bmhd->bnhd', a, v).reshape(B, N, HIDDEN)
        return o @ Wo.T + bo

    def _L2_gnn_ref(hidden_state, adjacency_matrix, Wl, bl, Ws, bs, Wr, br, ln_w, ln_b):
        import jax, jax.numpy as jnp
        import numpy as np
        LN_EPS = 1e-12

        def _digcn_forward(hidden_state, adjacency_matrix, Wl, bl, Ws, bs, Wr, br, ln_w, ln_b):
            B, S, D = hidden_state.shape
            temper = jnp.asarray(D, jnp.float32) ** 0.5
            i = jnp.arange(S)
            upper = (i[None, :] > i[:, None]).astype(hidden_state.dtype)
            lower = (i[None, :] < i[:, None]).astype(hidden_state.dtype)

            def layer(h, params):
                wl, b_l, ws, b_s, wr, b_r, g, beta = params
                u = jnp.einsum('bid,bjd->bij', h, h) / temper
                a = jax.nn.softmax(u, axis=-1)
                delta = a * adjacency_matrix
                attn = delta / (jnp.sum(delta, axis=-1, keepdims=True) + 1e-10)
                hl = h @ wl.T + b_l
                hs = h @ ws.T + b_s
                hr = h @ wr.T + b_r
                diag_a = jnp.diagonal(attn, axis1=1, axis2=2)
                ctx = jnp.einsum('bij,bjd->bid', attn * upper, hl) + diag_a[..., None] * hs + jnp.einsum('bij,bjd->bid', attn * lower, hr)
                mean = ctx.mean(-1, keepdims=True)
                var = ctx.var(-1, keepdims=True)
                o = (ctx - mean) / jnp.sqrt(var + LN_EPS) * g + beta
                return (jax.nn.relu(o), None)
            out, _ = jax.lax.scan(layer, hidden_state, (Wl, bl, Ws, bs, Wr, br, ln_w, ln_b))
            return out
        return _digcn_forward(hidden_state, adjacency_matrix, Wl, bl, Ws, bs, Wr, br, ln_w, ln_b)

    def _L3_gnn_ref(x, spatial_encoding, edge_encoding, Wq, Wk, Wv, bv, Wo, bo):
        import jax, jax.numpy as jnp
        import numpy as np
        NUM_HEADS = 12
        HIDDEN = 384
        HEAD = HIDDEN // NUM_HEADS
        B, N = (16, 256)
        b, n, h = x.shape
        scale = jnp.asarray(HIDDEN, x.dtype) ** (-0.5)
        q = (x @ Wq.T).reshape(b, n, NUM_HEADS, HEAD)
        k = (x @ Wk.T).reshape(b, n, NUM_HEADS, HEAD)
        v = (x @ Wv.T + bv).reshape(b, n, NUM_HEADS, HEAD)
        bias = (spatial_encoding + edge_encoding)[:, None]
        scores = jnp.einsum('bqhd,bkhd->bhqk', q, k) * scale + bias
        row_nonzero = jnp.any(scores != 0, axis=-1, keepdims=True)
        scores = jnp.where(row_nonzero, scores, -jnp.inf)
        p = jax.nn.softmax(scores, axis=-1)
        p = jnp.nan_to_num(p)
        out = jnp.einsum('bhqk,bkhd->bqhd', p, v).reshape(b, n, h)
        return out @ Wo.T + bo
    x = _layernorm(x + _L0_gnn_ref(x, adj, L0_gnn_Wq, L0_gnn_bq, L0_gnn_Wk, L0_gnn_bk, L0_gnn_Wv, L0_gnn_bv, L0_gnn_beta), axis=-1)
    x = _layernorm(x + _L1_gnn_ref(x, adj, L1_gnn_Wq, L1_gnn_Wk, L1_gnn_Wv, L1_gnn_bv, L1_gnn_Wo, L1_gnn_bo), axis=-1)
    x = _layernorm(x + _L2_gnn_ref(x, adj, L2_gnn_Wl, L2_gnn_bl, L2_gnn_Ws, L2_gnn_bs, L2_gnn_Wr, L2_gnn_br, L2_gnn_ln_w, L2_gnn_ln_b), axis=-1)
    x = _layernorm(x + _L3_gnn_ref(x, adj, adj, L3_gnn_Wq, L3_gnn_Wk, L3_gnn_Wv, L3_gnn_bv, L3_gnn_Wo, L3_gnn_bo), axis=-1)
    return x

_drawn_inputs = setup_inputs


def setup_inputs(seed=0):
    import zlib

    import numpy as np

    out = dict(_drawn_inputs(seed))
    spreads = {'L0_gnn_bq': (0.0, 0.1),
     'L0_gnn_bk': (0.0, 0.8),
     'L0_gnn_bv': (0.0, 0.1),
     'L2_gnn_bl': (0.0, 0.1),
     'L2_gnn_bs': (0.0, 0.315),
     'L2_gnn_br': (0.0, 0.1),
     'L2_gnn_ln_w': (1.0, 0.2),
     'L2_gnn_ln_b': (0.0, 0.1)}
    factors = {'L1_gnn_bv': 3.088,
     'L1_gnn_bo': 3.394,
     'L3_gnn_Wq': 8.0,
     'L3_gnn_Wk': 8.0,
     'L3_gnn_bv': 6.292,
     'L3_gnn_bo': 2.988}
    for name, (base, spread) in spreads.items():
        noise = np.random.default_rng([zlib.crc32(name.encode()), seed]).standard_normal(out[name].shape)
        drawn = base * np.exp(spread * noise) if base else spread * noise
        out[name] = jnp.asarray(drawn.astype(out[name].dtype))
    for name, factor in factors.items():
        out[name] = (out[name] * factor).astype(out[name].dtype)
    return out
```

```python
from contextlib import ExitStack

import concourse.bass as bass
from concourse import mybir

P = 128
B, N, D, H = 32, 256, 384, 12
HD = D // H
GP = 2
PAIRS = B // GP
QT = N // P
T = GP * QT
TOK = GP * N
KC = D // P
J = P // HD
NH = GP * H
GROUPS = H // J
RING = 4
NPT = 8
NPB = 3
MASKED = 9.0e15
FMAX = 3.4e38
LN_EPS, L2_LN_EPS, L2_SUM_EPS = 1e-5, 1e-12, 1e-10
RSQRT_MAGIC = float(0x5F3759DF)
NEWTON = 4

ALU = mybir.AluOpType
ACT = mybir.ActivationFunctionType
F32 = mybir.dt.float32
F32R = mybir.dt.float32r
I32 = mybir.dt.int32
AX = mybir.AxisListType

STATISTICS = 2 * QT + 3 + 3 * NEWTON

LAG_T, LAG_PV, LAG_NAT, LAG_ONT, LAG_OUT = 2, 4, 6, 7, 8


class Sem:

    def __init__(self, handle, credit):
        self.h, self.credit, self.base, self.per = handle, credit, credit, 0

    def at(self, i, k):
        return i * self.per + (self.base + k)


def wait_apart(eng, s, value):
    eng.wait_ge(s.h, value)
    eng.nop(nofuse=True)


class Layer:

    def __init__(self, n):
        self.n = n
        self.attn = n != 2
        self.proj = n in (1, 3)
        if n == 0:
            self.mats = ["L0_gnn_Wk", "L0_gnn_Wq", "L0_gnn_Wv"]
            self.scale = HD ** -0.5
        elif n == 2:
            self.mats = [f"L2_gnn_{m}{s}" for s in (0, 1) for m in ("Wl", "Ws", "Wr")]
            self.scale = D ** -0.5
        else:
            self.mats = [f"L{n}_gnn_{m}" for m in ("Wk", "Wq", "Wv", "Wo")]
            self.scale = D ** -0.5
        if self.attn:
            self.uses = 3 * KC + T + GP * GROUPS + T + (2 * T if self.proj else 0)
            self.steps = GP * (QT + STATISTICS + (3 if self.proj else 1)) + (NH if self.proj else 0)
            self.on_use = [3 * KC + T + GROUPS + QT, 3 * KC + T + 2 * GROUPS + 4 * QT]
        else:
            self.uses = 2 * (KC + 3 * T + GP + T)
            self.h_steps = 5 * T + GP * (4 * QT + STATISTICS)
            self.steps = 2 * self.h_steps + GP * STATISTICS
        self.pad = -self.uses % RING
        self.n_bias = {0: 4, 1: 2, 2: 10, 3: 2}[n]

    def max_step(self, sub, t):
        return sub * self.h_steps + 2 * (t + 1)

    def alloc(self, sb):
        n = f"L{self.n}_"
        self.x, self.res = sb(n + "x", [P, T, D]), sb(n + "res", [P, T, D])
        self.adj, self.edge = sb(n + "adj", [P, T, N]), sb(n + "edge", [P, T, N])
        self.y = sb(n + "y", [P, T, D])
        self.stage = sb(n + "stage", [P, 2, KC, D])
        self.w_hi = sb(n + "w_hi", [P, len(self.mats), KC, D], F32R)
        self.w_lo = sb(n + "w_lo", [P, len(self.mats), KC, D], F32R)
        self.xT = sb(n + "xT", [P, 2, KC, TOK], F32R)
        self.stats, self.mv = sb(n + "stats", [P, QT, 6]), sb(n + "mv", [P, QT, 2])
        self.var, self.half = sb(n + "var", [P, QT]), sb(n + "half", [P, QT], I32)
        self.rstd, self.tmp = sb(n + "rstd", [P, QT]), sb(n + "tmp", [P, QT])
        self.negmax, self.total = sb(n + "negmax", [P, NH, QT]), sb(n + "total", [P, NH, QT])
        self.rz = sb(n + "rz", [P, NH, QT])
        self.probs = sb(n + "probs", [P, NPB if self.attn else 4, QT if self.attn else 1, N])
        if self.attn:
            self.k_parts = sb(n + "k_parts", [P, 2, KC, TOK], F32R)
            self.q_parts = sb(n + "q_parts", [P, 2, KC, TOK], F32R)
            self.k_stack = sb(n + "k_stack", [3 * HD, J, KC, TOK], F32R)
            self.q_stack = sb(n + "q_stack", [3 * HD, J, KC, TOK], F32R)
            self.v = sb(n + "v", [P, T, D])
            self.v_bias = sb(n + "v_bias", [P, D])
            self.shifted = sb(n + "shifted", [P, 2, QT, N])
            self.pT = sb(n + "pT", [P, NPT, QT, N])
            self.oT = sb(n + "oT", [P, GROUPS, N])
            self.o = sb(n + "o", [P, QT, D])
            self.neg_beta = sb(n + "neg_beta", [P, 1])
            self.kq_bias = sb(n + "kq_bias", [P, 2, KC])
            if self.proj:
                self.absmax = sb(n + "absmax", [P, NH, QT])
                self.onT = sb(n + "onT", [P, 2, 2, KC, P], F32R)
                self.o_bias = sb(n + "o_bias", [P, D])
        else:
            self.h = sb(n + "h", [P, T, D])
            self.hp = sb(n + "hp", [P, 3, T, D])
            self.rows = sb(n + "rows", [P, 2, 5, D])
            self.delta = sb(n + "delta", [P, T, N])
            self.dT = sb(n + "dT", [P, 6, P])
            self.dsum, self.diag = sb(n + "dsum", [P, T]), sb(n + "diag", [P, T])
            self.rdel, self.scr = sb(n + "rdel", [P, T]), sb(n + "scr", [P, P])
            self.c = sb(n + "c", [P, QT, D])

    def bias_loads(self, w):
        n = f"L{self.n}_gnn_"

        def row(name):
            return w[name].rearrange("(a d) -> a d", a=1).broadcast_to([P, D])
        if self.n == 0:
            yield self.neg_beta[:], w[n + "beta"].rearrange("(a d) -> a d", a=1).broadcast_to([P, 1])
            yield self.v_bias[:], row(n + "bv")
            for kq, name in enumerate(("bk", "bq")):
                yield self.kq_bias[:, kq, :], w[n + name]
        elif self.n == 2:
            for s in range(2):
                for m, name in enumerate(("bl", "bs", "br", "ln_w", "ln_b")):
                    yield self.rows[:, s, m, :], w[n + name][s:s + 1, :].broadcast_to([P, D])
        else:
            yield self.v_bias[:], row(n + "bv")
            yield self.o_bias[:], row(n + "bo")


def build(nc, x_in, adj_in, w, out):
    ctx = ExitStack()
    with ctx:
        def sb(name, shape, dt=F32):
            return ctx.enter_context(nc.sbuf_tensor(name, shape, dt))

        sems = []

        def sem(name, credit=0):
            sems.append(Sem(ctx.enter_context(nc.semaphore(name)), credit))
            return sems[-1]

        ring = [ctx.enter_context(nc.psum_tensor(f"ring{r}", [P, 512], F32)) for r in range(RING)]
        sc_ps = [ctx.enter_context(nc.psum_tensor(f"scores{r}", [P, 512], F32)) for r in range(2)]
        pt_ps = [ctx.enter_context(nc.psum_tensor(f"probsT{r}", [P, 512], F32)) for r in range(2)]

        ident = sb("ident", [P, P])
        before = sb("before", [P, P])
        behind = sb("behind", [P, P])

        init_done = sem("init_done")
        x_loaded, adj_loaded = sem("x_loaded"), sem("adj_loaded")
        w_loaded = [sem(f"w_loaded{m}") for m in range(2)]
        w_hi, w_lo, b_loaded = sem("w_hi"), sem("w_lo"), sem("b_loaded")
        pool_step = sem("pool_step")
        kept = sem("kept")
        ring_full = sem("ring_full")
        ring_free = sem("ring_free", RING)
        hi_ready = sem("hi_ready")
        stacked = [sem(f"stacked{j}") for j in range(J)]
        sc_full = sem("sc_full")
        sc_read = sem("sc_read", 2)
        exp_done = sem("exp_done", 2)
        ptp_full = sem("ptp_full", NPB)
        pt_act, pt_dve = sem("pt_act", 1), sem("pt_dve", 1)
        dve_step = sem("dve_step")
        y_ready = sem("y_ready", 1)
        stored = sem("stored", 16)

        xs = [x_in] + [nc.dram_tensor(f"x_after{n}", (B * N, D), F32, kind="Internal").ap()
                       for n in range(3)] + [out]

        def nodes(ap):
            return ap.rearrange("(n t p) d -> n p t d", t=T, p=P)

        adj_v = adj_in.rearrange("(n b) (q p) k -> n p b q k", b=GP, p=P)

        layers = [Layer(n) for n in range(4)]
        for L in layers:
            with ExitStack() as own:
                L.alloc(lambda name, shape, dt=F32: own.enter_context(nc.sbuf_tensor(name, shape, dt)))

        def enter(L):
            x_loaded.per = adj_loaded.per = 16
            kept.per = 1
            ring_full.per = ring_free.per = L.uses + L.pad
            y_ready.per, stored.per = GP, 16 * GP
            dve_step.per = L.steps
            if L.attn:
                hi_ready.per = 3 * KC + (T if L.proj else 0)
                for s in stacked:
                    s.per = 16 * 6
                sc_full.per = sc_read.per = exp_done.per = ptp_full.per = NH
                pt_act.per = pt_dve.per = NH // 2
            else:
                hi_ready.per = 2 * KC
                sc_full.per = sc_read.per = exp_done.per = 2 * T

        def leave(L):
            for s in sems:
                s.base += PAIRS * s.per
                s.per = 0
            for m in range(2):
                w_loaded[m].base += 16 * len(L.mats[m::2])
            w_hi.base += len(L.mats)
            w_lo.base += len(L.mats)
            b_loaded.base += 16 * L.n_bias

        def begin():
            for s in sems:
                s.base, s.per = s.credit, 0

        block = ctx.enter_context(nc.Block())

        @block.sync
        def _(sp):
            begin()
            sp.sem_inc(stored.h, 16)
            for L in layers:
                enter(L)
                if L.n:
                    sp.wait_ge(stored.h, stored.base)
                for m, name in enumerate(L.mats):
                    if m >= 2:
                        sp.wait_ge(w_lo.h, w_lo.base + m - 1)
                    sp.dma_start(L.stage[:, m % 2, :, :],
                                 w[name].rearrange("(c p) n -> p c n", p=P)).then_inc(w_loaded[m % 2].h, 16)
                    if m == 0:
                        for dst, src in L.bias_loads(w):
                            sp.dma_start(dst, src).then_inc(b_loaded.h, 16)
                src_x, dst_x = nodes(xs[L.n]), nodes(xs[L.n + 1])

                def load(i):
                    sp.dma_start(L.x[:], src_x[i]).then_inc(x_loaded.h, 16)
                    sp.dma_start(L.adj[:].rearrange("p (b q) k -> p b q k", b=GP),
                                 adj_v[i]).then_inc(adj_loaded.h, 16)

                def pair(i, last):
                    if not last:
                        sp.wait_ge(kept.h, kept.at(i, 1))
                        sp.wait_ge(ring_full.h, ring_full.at(i, KC))
                        load(i + 1)
                    if L.attn:
                        for kq in range(2):
                            sp.wait_ge(ring_free.h, ring_free.at(i, KC * (2 + kq)))
                            src, dst, parts = ((L.k_parts, L.k_stack, (0, 0, 1)),
                                               (L.q_parts, L.q_stack, (0, 1, 0)))[kq]
                            for j in range(J):
                                for r, part in enumerate(parts):
                                    sp.dma_start(dst[HD * r:HD * r + HD, j, :, :].bitcast(F32),
                                                 src[HD * j:HD * j + HD, part, :, :].bitcast(F32)
                                                 ).then_inc(stacked[j].h, 16)
                    for b in range(GP):
                        sp.wait_ge(y_ready.h, y_ready.at(i, b + 1))
                        sp.dma_start(dst_x[i][:, QT * b:QT * b + QT, :],
                                     L.y[:, QT * b:QT * b + QT, :]).then_inc(stored.h, 16)

                load(0)
                with sp.Fori(0, PAIRS - 1) as i:
                    pair(i, False)
                pair(PAIRS - 1, True)
                leave(L)
            sp.wait_ge(stored.h, stored.base)

        @block.gpsimd
        def _(pool):
            begin()
            g = nc.gpsimd
            g.memset(ident[:], 0.0).then_inc(pool_step.h, 1)
            g.memset(before[:], 1.0).then_inc(pool_step.h, 1)
            g.memset(behind[:], 1.0).then_inc(pool_step.h, 1)
            pool.wait_ge(pool_step.h, 3)
            g.affine_select(out=ident[:], in_=ident[:], compare_op=ALU.not_equal, fill=1.0, base=0,
                            pattern=[[-1, P]], channel_multiplier=1).then_inc(init_done.h, 1)
            g.affine_select(out=before[:], in_=before[:], compare_op=ALU.is_gt, fill=0.0, base=0,
                            pattern=[[1, P]], channel_multiplier=-1).then_inc(init_done.h, 1)
            g.affine_select(out=behind[:], in_=behind[:], compare_op=ALU.is_gt, fill=0.0, base=0,
                            pattern=[[-1, P]], channel_multiplier=1).then_inc(init_done.h, 1)
            pool_step.base = 3
            for L in layers:
                enter(L)
                pool_step.per = 3 if L.n == 0 else 1
                if L.n == 0:
                    pool.wait_ge(b_loaded.h, b_loaded.base + 16 * L.n_bias)
                    g.tensor_scalar(L.neg_beta[:], L.neg_beta[:], -1.0, None, ALU.mult).then_inc(pool_step.h, 1)
                    pool_step.base += 1
                    pool.wait_ge(pool_step.h, pool_step.base)
                with pool.Fori(0, PAIRS) as i:
                    pool.wait_ge(x_loaded.h, x_loaded.at(i, 16))
                    pool.wait_ge(adj_loaded.h, adj_loaded.at(i, 16))
                    wait_apart(pool, y_ready, y_ready.at(i, 0))
                    g.tensor_copy(L.res[:], L.x[:]).then_inc(pool_step.h, 1)
                    if L.n == 0:
                        g.tensor_scalar(L.edge[:], L.adj[:], 0.0, MASKED, ALU.is_le, ALU.mult
                                        ).then_inc(pool_step.h, 1)
                        g.tensor_scalar(L.adj[:], L.adj[:], L.neg_beta[:], None, ALU.mult
                                        ).then_inc(pool_step.h, 1)
                        pool.wait_ge(pool_step.h, pool_step.at(i, 3))
                        g.tensor_tensor(L.edge[:], L.edge[:], L.adj[:], ALU.add).then_inc(kept.h, 1)
                    else:
                        f = {1: -1.0, 2: 1.0, 3: -2.0}[L.n]
                        wait_apart(pool, pool_step, pool_step.at(i, 1))
                        g.tensor_scalar(L.edge[:], L.adj[:], f, None, ALU.mult).then_inc(kept.h, 1)
                leave(L)

        @block.tensor
        def _(pe):
            begin()
            pe.sem_inc(ptp_full.h, NPB)
            pe.wait_ge(init_done.h, 3)
            t_ = nc.tensor

            def parts3(ps, lhsT, rhs, chunks, first=True, last=True):
                terms = [(c, a, b) for c in range(chunks) for a, b in ((0, 0), (0, 1), (1, 0))]
                for n, (c, a, b) in enumerate(terms):
                    mm = t_.matmul(ps, lhsT(a, c), rhs(b, c), start=first and n == 0,
                                   stop=last and n == len(terms) - 1)
                return mm

            for L in layers:
                enter(L)
                use = [0]

                def ring_use(i):
                    pe.wait_ge(ring_free.h, ring_free.at(i, use[0] + 1 - RING))
                    use[0] += 1
                    return ring[(use[0] - 1) % RING]

                def done(mm):
                    mm.then_inc(ring_full.h, 1 + (L.pad if use[0] == L.uses else 0))

                def w_part(m):
                    return lambda a, c: (L.w_hi, L.w_lo)[a][:, m, c, :]

                def transposes_x(i, src):
                    for c in range(KC):
                        ps = ring_use(i)
                        for t in range(T):
                            mm = t_.transpose(ps[:, P * t:P * t + P], src[:, t, P * c:P * c + P], ident[:])
                        done(mm)

                pe.wait_ge(w_lo.h, w_lo.base + len(L.mats))
                with pe.Fori(0, PAIRS) as i:
                    use[0] = 0
                    if L.attn:
                        pe.wait_ge(x_loaded.h, x_loaded.at(i, 16))
                        transposes_x(i, L.x)
                        pe.wait_ge(ring_free.h, ring_free.at(i, KC))
                        for m in range(2):
                            for c in range(KC):
                                ps = ring_use(i)
                                done(parts3(ps[:], lambda a, k: w_part(m)(a, k)[:, P * c:P * c + P],
                                            lambda b, k: L.xT[:, b, k, :], KC))
                        for t in range(T):
                            ps = ring_use(i)
                            done(parts3(ps[:, 0:D], lambda a, k: L.xT[:, a, k, P * t:P * t + P],
                                        w_part(2), KC))
                        for s in range(NH + LAG_OUT):
                            if s < NH:
                                b, h = divmod(s, H)
                                j, c = divmod(h, KC)
                                if b == 0 and c == 0:
                                    pe.wait_ge(stacked[j].h, stacked[j].at(i, 16 * 6))
                                pe.wait_ge(sc_read.h, sc_read.at(i, s + 1 - 2))
                                for q in range(QT):
                                    mm = t_.matmul(sc_ps[s % 2][:, N * q:N * q + N],
                                                   L.q_stack[:, j, c, N * b + P * q:N * b + P * q + P],
                                                   L.k_stack[:, j, c, N * b:N * b + N], start=True, stop=True)
                                mm.then_inc(sc_full.h, 1)
                            if LAG_T <= s < NH + LAG_T:
                                r = s - LAG_T
                                pe.wait_ge(exp_done.h, exp_done.at(i, r + 1))
                                ev = (pt_act, pt_dve)[r % 2]
                                pe.wait_ge(ev.h, ev.at(i, r // 2))
                                for kt in range(QT):
                                    for q in range(QT):
                                        mm = t_.transpose(pt_ps[r % 2][:, N * kt + P * q:N * kt + P * q + P],
                                                          L.probs[:, r % NPB, q, P * kt:P * kt + P], ident[:])
                                mm.then_inc(ptp_full.h, 1)
                            r = s - LAG_PV
                            if 0 <= r < NH and r % J == J - 1:
                                b, gr = divmod(r // J, GROUPS)
                                pe.wait_ge(pt_act.h, pt_act.at(i, r // 2 + 1))
                                pe.wait_ge(pt_dve.h, pt_dve.at(i, r // 2 + 1))
                                if r == J - 1:
                                    pe.wait_ge(ring_free.h, ring_free.at(i, 3 * KC + T))
                                ps = ring_use(i)
                                for kt in range(QT):
                                    for k in range(J):
                                        hh = J * gr + k
                                        mm = t_.matmul(ps[HD * k:HD * k + HD, 0:N],
                                                       L.v[:, QT * b + kt, HD * hh:HD * hh + HD],
                                                       L.pT[:, (H * b + hh) % NPT, kt, :],
                                                       start=kt == 0, stop=kt == QT - 1)
                                done(mm)
                            if s >= LAG_NAT and (s - LAG_NAT) % H == H - 1:
                                pe.wait_ge(ring_free.h, ring_free.at(i, use[0]))
                                for q in range(QT):
                                    ps = ring_use(i)
                                    for gr in range(GROUPS):
                                        mm = t_.transpose(ps[:, P * gr:P * gr + P],
                                                          L.oT[:, gr, P * q:P * q + P], ident[:])
                                    done(mm)
                            if L.proj and s >= LAG_ONT and (s - LAG_ONT) % H == H - 1:
                                pe.wait_ge(ring_free.h, ring_free.at(i, use[0]))
                                for q in range(QT):
                                    ps = ring_use(i)
                                    for c in range(KC):
                                        mm = t_.transpose(ps[:, P * c:P * c + P],
                                                          L.o[:, q, P * c:P * c + P], ident[:])
                                    done(mm)
                            if L.proj and s >= LAG_OUT and (s - LAG_OUT) % H == H - 1:
                                pe.wait_ge(ring_free.h, ring_free.at(i, use[0]))
                                for q in range(QT):
                                    ps = ring_use(i)
                                    done(parts3(ps[:, 0:D], lambda a, k: L.onT[:, q, a, k, :],
                                                w_part(3), KC))
                    else:
                        for sub in range(2):
                            if sub == 0:
                                pe.wait_ge(x_loaded.h, x_loaded.at(i, 16))
                            else:
                                pe.wait_ge(dve_step.h, dve_step.at(i, L.h_steps))
                            transposes_x(i, L.x if sub == 0 else L.h)
                            pe.wait_ge(ring_free.h, ring_free.at(i, use[0]))
                            for t in range(T):
                                b = t // QT
                                pe.wait_ge(exp_done.h, exp_done.at(i, T * sub + t + 1 - 2))
                                parts3(sc_ps[t % 2][:, 0:N], lambda a, k: L.xT[:, a, k, P * t:P * t + P],
                                       lambda bb, k: L.xT[:, bb, k, N * b:N * b + N], KC
                                       ).then_inc(sc_full.h, 1)
                            for t in range(T):
                                for m in range(3):
                                    ps = ring_use(i)
                                    done(parts3(ps[:, 0:D], lambda a, k: L.xT[:, a, k, P * t:P * t + P],
                                                w_part(3 * sub + m), KC))
                            for b in range(GP):
                                pe.wait_ge(sc_read.h, sc_read.at(i, T * sub + QT * b + QT))
                                ps = ring_use(i)
                                for jt in range(QT):
                                    for it in range(QT):
                                        mm = t_.transpose(ps[:, N * jt + P * it:N * jt + P * it + P],
                                                          L.delta[:, QT * b + it, P * jt:P * jt + P], ident[:])
                                done(mm)
                                pe.wait_ge(ring_free.h, ring_free.at(i, use[0]))
                                for it in range(QT):
                                    ps = ring_use(i)
                                    for n, (blk, m, jt) in enumerate(
                                            [((0, 0, 0), (1, 0, 1), (3, 2, 0)),
                                             ((2, 0, 1), (4, 2, 0), (5, 2, 1))][it]):
                                        mm = t_.matmul(ps[:, 0:D], L.dT[:, blk, :], L.hp[:, m, QT * b + jt, :],
                                                       start=n == 0, stop=n == 2)
                                    done(mm)
                leave(L)

        @block.scalar
        def _(act):
            begin()
            act.sem_inc(exp_done.h, 2)
            act.sem_inc(pt_act.h, 1)
            a_ = nc.scalar
            for L in layers:
                enter(L)
                for m in range(len(L.mats)):
                    act.wait_ge(w_loaded[m % 2].h, w_loaded[m % 2].base + 16 * (m // 2 + 1))
                    kq = L.attn and m < 2
                    f = -L.scale if L.attn and m == 1 else 1.0
                    for c in range(KC):
                        src, dst = L.stage[:, m % 2, c, :], L.w_hi[:, m, c, :]
                        if kq:
                            for k in range(KC):
                                mm = a_.activation(dst[:, P * k:P * k + P].rearrange("p (j d) -> p j d", j=J),
                                                   src.rearrange("p (j c d) -> p c j d", j=J, c=KC)[:, k],
                                                   ACT.Copy, scale=f)
                        else:
                            mm = a_.activation(dst, src, ACT.Copy, scale=f)
                    mm.then_inc(w_hi.h, 1)
                if L.n == 0:
                    act.wait_ge(b_loaded.h, b_loaded.base + 16 * L.n_bias)
                    act.wait_ge(w_lo.h, w_lo.base + len(L.mats))

                def copy_high(i, r, dst, bias=None):
                    act.wait_ge(ring_full.h, ring_full.at(i, r + 1))
                    src = ring[r % RING][:, 0:dst.shape[1]]
                    if bias is None:
                        a_.activation(dst, src, ACT.Copy).then_inc(hi_ready.h, 1)
                    else:
                        a_.activation(dst, src, ACT.Identity, bias=bias).then_inc(hi_ready.h, 1)

                with act.Fori(0, PAIRS) as i:
                    if L.attn:
                        for c in range(KC):
                            copy_high(i, c, L.xT[:, 0, c, :])
                        for m in range(2):
                            for c in range(KC):
                                copy_high(i, KC * (1 + m) + c, (L.k_parts, L.q_parts)[m][:, 0, c, :],
                                          L.kq_bias[:, m, c:c + 1] if L.n == 0 else None)
                        for s in range(NH + LAG_OUT):
                            if s < NH:
                                act.wait_ge(sc_read.h, sc_read.at(i, s + 1))
                                act.wait_ge(ptp_full.h, ptp_full.at(i, s + 1 - NPB))
                                for q in range(QT):
                                    mm = a_.activation(L.probs[:, s % NPB, q, :], L.shifted[:, s % 2, q, :],
                                                       ACT.Exp, scale=-1.0, bias=L.negmax[:, s, q:q + 1],
                                                       accum_out=L.total[:, s, q:q + 1])
                                mm.then_inc(exp_done.h, 1)
                            r = s - LAG_T
                            if 0 <= r < NH and r % 2 == 0:
                                act.wait_ge(ptp_full.h, ptp_full.at(i, r + 1))
                                a_.activation(L.pT[:, r % NPT, :, :].rearrange("p k n -> p (k n)"),
                                              pt_ps[0][:], ACT.Copy).then_inc(pt_act.h, 1)
                            if L.proj and s >= LAG_ONT and (s - LAG_ONT) % H == H - 1:
                                first = L.on_use[(s - LAG_ONT) // H]
                                for q in range(QT):
                                    copy_high(i, first + q, L.onT[:, q, 0, :, :].rearrange("p c n -> p (c n)"))
                    else:
                        for sub in range(2):
                            for c in range(KC):
                                copy_high(i, sub * (L.uses // 2) + c, L.xT[:, 0, c, :])
                            for t in range(T):
                                act.wait_ge(dve_step.h, dve_step.at(i, L.max_step(sub, t)))
                                a_.activation(L.probs[:, t, 0, :], sc_ps[t % 2][:, 0:N], ACT.Exp,
                                              scale=L.scale, bias=L.negmax[:, t, 0:1],
                                              accum_out=L.total[:, t, 0:1]).then_inc(exp_done.h, 1)
                leave(L)

        @block.vector
        def _(dve):
            begin()
            dve.sem_inc(ring_free.h, RING)
            dve.sem_inc(sc_read.h, 2)
            dve.sem_inc(pt_dve.h, 1)
            dve.sem_inc(y_ready.h, 1)
            v_ = nc.vector
            dve.wait_ge(init_done.h, 3)
            for L in layers:
                enter(L)
                for m in range(len(L.mats)):
                    dve.wait_ge(w_hi.h, w_hi.base + m + 1)
                    kq = L.attn and m < 2
                    f = -L.scale if L.attn and m == 1 else 1.0
                    if L.n == 0 and m == 1:
                        dve.wait_ge(b_loaded.h, b_loaded.base + 16 * L.n_bias)
                        v_.tensor_scalar(L.kq_bias[:, 1, :], L.kq_bias[:, 1, :], f, None, ALU.mult)
                    for c in range(KC):
                        src, hi, dst = L.stage[:, m % 2, c, :], L.w_hi[:, m, c, :], L.w_lo[:, m, c, :]
                        if kq:
                            for k in range(KC):
                                sl = slice(P * k, P * k + P)
                                mm = v_.scalar_tensor_tensor(
                                    out=dst[:, sl].rearrange("p (j d) -> p j d", j=J),
                                    in0=src.rearrange("p (j c d) -> p c j d", j=J, c=KC)[:, k], scalar=f,
                                    in1=hi[:, sl].bitcast(F32).rearrange("p (j d) -> p j d", j=J),
                                    op0=ALU.mult, op1=ALU.subtract)
                        else:
                            mm = v_.scalar_tensor_tensor(out=dst, in0=src, scalar=f, in1=hi.bitcast(F32),
                                                         op0=ALU.mult, op1=ALU.subtract)
                    mm.then_inc(w_lo.h, 1)
                dve.wait_ge(b_loaded.h, b_loaded.base + 16 * L.n_bias)
                dve.wait_ge(w_lo.h, w_lo.base + len(L.mats))
                use, step, hi_n = [0], [0], [0]

                def step_done(i, ins, wait=True):
                    step[0] += 1
                    ins.then_inc(dve_step.h, 1)
                    if wait:
                        dve.wait_ge(dve_step.h, dve_step.at(i, step[0]))

                def ring_use(i):
                    dve.wait_ge(ring_full.h, ring_full.at(i, use[0] + 1))
                    use[0] += 1
                    return ring[(use[0] - 1) % RING]

                def freed(ins):
                    ins.then_inc(ring_free.h, 1 + (L.pad if use[0] == L.uses else 0))

                def low_part(i, dst, hi, bias=None):
                    ps = ring_use(i)
                    hi_n[0] += 1
                    dve.wait_ge(hi_ready.h, hi_ready.at(i, hi_n[0]))
                    src, hi = ps[:, 0:dst.shape[1]], hi.bitcast(F32)
                    if bias is None:
                        freed(v_.tensor_tensor(dst, src, hi, ALU.subtract))
                    else:
                        freed(v_.scalar_tensor_tensor(out=dst, in0=src, scalar=bias, in1=hi,
                                                      op0=ALU.add, op1=ALU.subtract))

                def rsqrt(i, eps):
                    step_done(i, v_.tensor_scalar(L.var[:], L.mv[:, :, 1], eps, None, ALU.add))
                    step_done(i, v_.tensor_scalar(L.half[:], L.var[:].bitcast(I32), 1, None,
                                                  ALU.logical_shift_right))
                    step_done(i, v_.tensor_scalar(L.rstd[:].bitcast(I32), L.half[:], -1.0, RSQRT_MAGIC,
                                                  ALU.mult, ALU.add))
                    for _ in range(NEWTON):
                        step_done(i, v_.scalar_tensor_tensor(out=L.tmp[:], in0=L.rstd[:], scalar=-0.5,
                                                             in1=L.rstd[:], op0=ALU.mult, op1=ALU.mult))
                        step_done(i, v_.tensor_tensor(L.tmp[:], L.tmp[:], L.var[:], ALU.mult))
                        step_done(i, v_.scalar_tensor_tensor(out=L.rstd[:], in0=L.tmp[:], scalar=1.5,
                                                             in1=L.rstd[:], op0=ALU.add, op1=ALU.mult))

                def statistics(i, tiles, eps):
                    for q, tile in enumerate(tiles):
                        step_done(i, v_.bn_stats(L.stats[:, q, :], tile), wait=False)
                    wait_apart(dve, dve_step, dve_step.at(i, step[0]))
                    for q in range(QT):
                        step_done(i, v_.bn_aggr(L.mv[:, q, :], L.stats[:, q, :]), wait=q == QT - 1)
                    rsqrt(i, eps)

                def layer_norm(i, b):
                    statistics(i, [L.y[:, QT * b + q, :] for q in range(QT)], LN_EPS)
                    for q in range(QT):
                        ins = v_.tensor_scalar(L.y[:, QT * b + q, :], L.y[:, QT * b + q, :],
                                               L.mv[:, q, 0:1], L.rstd[:, q:q + 1], ALU.subtract, ALU.mult)
                    ins.then_inc(y_ready.h, 1)

                def y_free(i, b):
                    if b == 0:
                        dve.wait_ge(stored.h, stored.at(i, 0))

                with dve.Fori(0, PAIRS) as i:
                    use[0] = step[0] = hi_n[0] = 0
                    if L.attn:
                        for c in range(KC):
                            low_part(i, L.xT[:, 1, c, :], L.xT[:, 0, c, :])
                        for m in range(2):
                            for c in range(KC):
                                kq = (L.k_parts, L.q_parts)[m]
                                low_part(i, kq[:, 1, c, :], kq[:, 0, c, :],
                                         L.kq_bias[:, m, c:c + 1] if L.n == 0 else None)
                        for t in range(T):
                            ps = ring_use(i)
                            freed(v_.tensor_tensor(L.v[:, t, :], ps[:, 0:D], L.v_bias[:], ALU.add))
                        dve.wait_ge(kept.h, kept.at(i, 1))
                        for s in range(NH + LAG_OUT):
                            if s < NH:
                                b = s // H
                                dve.wait_ge(sc_full.h, sc_full.at(i, s + 1))
                                wait_apart(dve, exp_done, exp_done.at(i, s + 1 - 2))
                                for q in range(QT):
                                    ins = v_.tensor_tensor_reduce(
                                        L.shifted[:, s % 2, q, :], sc_ps[s % 2][:, N * q:N * q + N],
                                        L.edge[:, QT * b + q, :], 1.0, FMAX, ALU.add, ALU.min,
                                        L.negmax[:, s, q:q + 1])
                                ins.then_inc(sc_read.h, 1)
                                if L.proj:
                                    dve.wait_ge(sc_read.h, sc_read.at(i, s + 1))
                                    step_done(i, v_.tensor_reduce(L.absmax[:, s, :], L.shifted[:, s % 2, :, :],
                                                                  AX.X, ALU.max, apply_absolute_value=True),
                                              wait=False)
                            r = s - LAG_T
                            if 0 <= r < NH and r % 2 == 1:
                                dve.wait_ge(ptp_full.h, ptp_full.at(i, r + 1))
                                v_.tensor_copy(L.pT[:, r % NPT, :, :].rearrange("p k n -> p (k n)"),
                                               pt_ps[1][:]).then_inc(pt_dve.h, 1)
                            r = s - LAG_PV
                            if 0 <= r < NH and r % J == J - 1:
                                ps = ring_use(i)
                                freed(v_.tensor_copy(L.oT[:, r // J % GROUPS, :], ps[:, 0:N]))
                            if s >= LAG_NAT and (s - LAG_NAT) % H == H - 1:
                                b = (s - LAG_NAT) // H
                                hs = slice(H * b, H * b + H)
                                dve.wait_ge(exp_done.h, exp_done.at(i, H * b + H))
                                if b == 0:
                                    y_free(i, b)
                                step_done(i, v_.reciprocal(L.rz[:, hs, :], L.total[:, hs, :]), wait=False)
                                if L.proj:
                                    step_done(i, v_.tensor_scalar(L.absmax[:, hs, :], L.absmax[:, hs, :], 0.0,
                                                                  None, ALU.is_gt))
                                    step_done(i, v_.tensor_tensor(L.rz[:, hs, :], L.rz[:, hs, :],
                                                                  L.absmax[:, hs, :], ALU.mult), wait=False)
                                dve.wait_ge(dve_step.h, dve_step.at(i, step[0]))
                                for q in range(QT):
                                    ps = ring_use(i)
                                    freed(v_.tensor_tensor(
                                        L.o[:, q, :].rearrange("p (h d) -> p h d", h=H),
                                        ps[:, 0:D].rearrange("p (h d) -> p h d", h=H),
                                        L.rz[:, hs, q:q + 1].broadcast_to([P, H, HD]), ALU.mult))
                                if not L.proj:
                                    for q in range(QT):
                                        dve.wait_ge(ring_free.h, ring_free.at(i, use[0] - QT + q + 1))
                                        step_done(i, v_.tensor_tensor(L.y[:, QT * b + q, :], L.o[:, q, :],
                                                                      L.res[:, QT * b + q, :], ALU.add),
                                                  wait=q == QT - 1)
                                    layer_norm(i, b)
                            if L.proj and s >= LAG_ONT and (s - LAG_ONT) % H == H - 1:
                                for q in range(QT):
                                    low_part(i, L.onT[:, q, 1, :, :].rearrange("p c n -> p (c n)"),
                                             L.onT[:, q, 0, :, :].rearrange("p c n -> p (c n)"))
                                b = (s - LAG_ONT) // H
                                for q in range(QT):
                                    step_done(i, v_.tensor_tensor(L.y[:, QT * b + q, :], L.res[:, QT * b + q, :],
                                                                  L.o_bias[:], ALU.add), wait=q == QT - 1)
                            if L.proj and s >= LAG_OUT and (s - LAG_OUT) % H == H - 1:
                                b = (s - LAG_OUT) // H
                                for q in range(QT):
                                    ps = ring_use(i)
                                    freed(v_.tensor_tensor(L.y[:, QT * b + q, :], ps[:, 0:D],
                                                           L.y[:, QT * b + q, :], ALU.add))
                                dve.wait_ge(ring_free.h, ring_free.at(i, use[0] + (L.pad if use[0] == L.uses else 0)))
                                layer_norm(i, b)
                    else:
                        for sub in range(2):
                            for c in range(KC):
                                low_part(i, L.xT[:, 1, c, :], L.xT[:, 0, c, :])
                            if sub == 0:
                                dve.wait_ge(kept.h, kept.at(i, 1))
                            for t in range(T):
                                n = T * sub + t
                                dve.wait_ge(sc_full.h, sc_full.at(i, n + 1))
                                step_done(i, v_.tensor_reduce(L.dsum[:, t:t + 1], sc_ps[t % 2][:, 0:N],
                                                              AX.X, ALU.max))
                                step_done(i, v_.tensor_scalar(L.negmax[:, t, 0:1], L.dsum[:, t:t + 1],
                                                              -L.scale, None, ALU.mult), wait=False)
                                assert step[0] == L.max_step(sub, t)
                            for t in range(T):
                                n = T * sub + t
                                for m in range(3):
                                    ps = ring_use(i)
                                    freed(v_.tensor_tensor(L.hp[:, m, t, :], ps[:, 0:D],
                                                           L.rows[:, sub, m, :], ALU.add))
                                dve.wait_ge(exp_done.h, exp_done.at(i, n + 1))
                                v_.tensor_tensor_reduce(L.delta[:, t, :], L.probs[:, t, 0, :], L.edge[:, t, :],
                                                        1.0, 0.0, ALU.mult, ALU.add,
                                                        L.dsum[:, t:t + 1]).then_inc(sc_read.h, 1)
                                dve.wait_ge(sc_read.h, sc_read.at(i, n + 1))
                                q = t % QT
                                step_done(i, v_.tensor_tensor_reduce(
                                    L.scr[:], L.delta[:, t, P * q:P * q + P], ident[:], 1.0, 0.0,
                                    ALU.mult, ALU.add, L.diag[:, t:t + 1]), wait=False)
                                step_done(i, v_.scalar_tensor_tensor(
                                    out=L.rdel[:, t:t + 1], in0=L.total[:, t, 0:1], scalar=L2_SUM_EPS,
                                    in1=L.dsum[:, t:t + 1], op0=ALU.mult, op1=ALU.add))
                                step_done(i, v_.reciprocal(L.rdel[:, t:t + 1], L.rdel[:, t:t + 1]), wait=False)
                            dve.wait_ge(ring_free.h, ring_free.at(i, use[0]))
                            for b in range(GP):
                                ps = ring_use(i)

                                def block_of(jt, it):
                                    return ps[:, N * jt + P * it:N * jt + P * it + P]
                                v_.tensor_tensor(L.dT[:, 0, :], block_of(0, 0), behind[:], ALU.mult)
                                v_.tensor_tensor(L.dT[:, 2, :], block_of(1, 1), behind[:], ALU.mult)
                                v_.tensor_tensor(L.dT[:, 3, :], block_of(0, 0), before[:], ALU.mult)
                                v_.tensor_tensor(L.dT[:, 5, :], block_of(1, 1), before[:], ALU.mult)
                                v_.tensor_copy(L.dT[:, 1, :], block_of(1, 0))
                                freed(v_.tensor_copy(L.dT[:, 4, :], block_of(0, 1)))
                                for q in range(QT):
                                    t = QT * b + q
                                    ps = ring_use(i)
                                    ins = v_.scalar_tensor_tensor(
                                        out=L.c[:, q, :], in0=L.hp[:, 1, t, :], scalar=L.diag[:, t:t + 1],
                                        in1=ps[:, 0:D], op0=ALU.mult, op1=ALU.add)
                                    freed(ins)
                                    dve.wait_ge(ring_free.h, ring_free.at(i, use[0] + (L.pad if use[0] == L.uses else 0)))
                                    step_done(i, v_.tensor_scalar(L.c[:, q, :], L.c[:, q, :], L.rdel[:, t:t + 1],
                                                                  None, ALU.mult), wait=q == QT - 1)
                                statistics(i, [L.c[:, q, :] for q in range(QT)], L2_LN_EPS)
                                for q in range(QT):
                                    step_done(i, v_.scalar_tensor_tensor(
                                        out=L.c[:, q, :], in0=L.c[:, q, :], scalar=L.mv[:, q, 0:1],
                                        in1=L.rows[:, sub, 3, :], op0=ALU.subtract, op1=ALU.mult), wait=q == QT - 1)
                                for q in range(QT):
                                    step_done(i, v_.scalar_tensor_tensor(
                                        out=L.c[:, q, :], in0=L.c[:, q, :], scalar=L.rstd[:, q:q + 1],
                                        in1=L.rows[:, sub, 4, :], op0=ALU.mult, op1=ALU.add), wait=q == QT - 1)
                                if sub == 0:
                                    for q in range(QT):
                                        step_done(i, v_.tensor_scalar(L.h[:, QT * b + q, :], L.c[:, q, :], 0.0,
                                                                      None, ALU.max), wait=False)
                                    if b == GP - 1:
                                        assert step[0] == L.h_steps, step[0]
                                else:
                                    y_free(i, b)
                                    for q in range(QT):
                                        step_done(i, v_.scalar_tensor_tensor(
                                            out=L.y[:, QT * b + q, :], in0=L.c[:, q, :], scalar=0.0,
                                            in1=L.res[:, QT * b + q, :], op0=ALU.max, op1=ALU.add),
                                            wait=q == QT - 1)
                                    layer_norm(i, b)
                    assert step[0] == L.steps and use[0] == L.uses, (L.n, step[0], use[0], L.uses)
                leave(L)


def kernel(**inputs):
    import numpy as np
    import concourse.bacc as bacc
    from concourse.bass_utils import run_bass_kernel_spmd

    nc = bacc.Bacc("TRN2", target_bir_lowering=False, num_devices=1)
    arrays, aps = {}, {}

    def give(name, a):
        a = np.ascontiguousarray(a)
        arrays[name] = a
        aps[name] = nc.dram_tensor(name, a.shape, mybir.dt.from_np(a.dtype), kind="ExternalInput").ap()

    give("x", np.asarray(inputs["x"]).reshape(B * N, D))
    give("adj", inputs["adj"])
    for name, a in inputs.items():
        a = np.asarray(a)
        if name in ("x", "adj"):
            continue
        if name.startswith("L2_gnn_W"):
            for s in range(2):
                give(f"{name}{s}", a[s].T)
        elif name[:7] in ("L1_gnn_", "L3_gnn_") and name[7] == "W":
            give(name, a.T)
        elif name in ("L0_gnn_bk", "L0_gnn_bq"):
            give(name, a.reshape(J, KC, HD).transpose(0, 2, 1).reshape(P, KC))
        elif a.ndim == 0:
            give(name, a.reshape(1))
        else:
            give(name, a)
    out = nc.dram_tensor("out", (B * N, D), F32, kind="ExternalOutput").ap()
    build(nc, aps["x"], aps["adj"], aps, out)
    r = run_bass_kernel_spmd(nc, [arrays], core_ids=[0])
    return r.results[0]["out"].reshape(B, N, D)
```

```python
from contextlib import ExitStack

import concourse.bass as bass
from concourse import mybir

P = 128
B, N, D, H = 32, 256, 384, 12
HD = D // H
GP = 2
PAIRS = B // GP
QT = N // P
T = GP * QT
TOK = GP * N
KC = D // P
J = P // HD
NH = GP * H
GROUPS = H // J
NPT = 8
NPB = 3
NSH = 3
SUBS = 2
UNITS = GP * SUBS
MASKED = 9.0e15
FMAX = 3.4e38
LN_EPS, L2_LN_EPS, L2_SUM_EPS = 1e-5, 1e-12, 1e-10
RSQRT_MAGIC = float(0x5F3759DF)
NEWTON = 3

ALU = mybir.AluOpType
ACT = mybir.ActivationFunctionType
F32 = mybir.dt.float32
F32R = mybir.dt.float32r
I32 = mybir.dt.int32
AX = mybir.AxisListType

STATISTICS = 2 * QT + 3 + 3 * NEWTON
ESTIMATE = 3
BEGUN = 2 * QT + ESTIMATE

LAG_T, LAG_PV = 2, 4
NAT, ONT = 4, 9
OUT, SUM, ESTIMATED, APPLY = 0, 1, 4, 7
KEEP_RES, KEEP_EDGE = 4, 2
FOLDS = 4
FOLDED = N // 4

PROJ_AT = {0: (0, 1), 1: (2,), 2: (3, 4), 3: (5,), 4: (6,), 5: (7,), 6: (8,), 8: (9,), 10: (10,)}
PROJ_USES = 3 * KC + QT
K_USE, Q_USE, V_USE = KC, 2 * KC, 3 * KC

HEADS_USE = {False: (3, 4, 5), True: (5, 8, 11)}
END_USE = {False: (6, 7), True: (12, 13, 15, 16, 18, 19)}
ATT_USES = {False: 5, True: 9}


class Sem:

    def __init__(self, handle, credit):
        self.h, self.credit, self.base, self.per = handle, credit, credit, 0

    def at(self, unit, k):
        i, per_iteration, n = unit
        return i * (per_iteration * self.per) + (self.base + n * self.per + k)


def graph(i, n):
    return (i, GP, n)


def of_parity(i, n):
    return (i, 1, n // GP)


def stage_unit(i, u):
    return (i, UNITS, u)


def wait_apart(eng, s, value):
    eng.wait_ge(s.h, value)
    eng.nop(nofuse=True)


class Layer:

    def __init__(self, n):
        self.n = n
        self.attn = n != 2
        self.proj = n in (1, 3)
        if n == 0:
            self.mats = ["L0_gnn_Wk", "L0_gnn_Wq", "L0_gnn_Wv"]
            self.scale = HD ** -0.5
        elif n == 2:
            self.mats = [f"L2_gnn_{m}{s}" for s in range(SUBS) for m in ("Wl", "Ws", "Wr")]
            self.scale = D ** -0.5
        else:
            self.mats = [f"L{n}_gnn_{m}" for m in ("Wk", "Wq", "Wv", "Wo")]
            self.scale = D ** -0.5
        if self.proj:
            self.steps = 3 + BEGUN
        elif self.attn:
            self.steps = 1 + QT + BEGUN
        else:
            self.sub_steps = [4 * QT + STATISTICS, 4 * QT + 2 * STATISTICS]
            self.steps = max(self.sub_steps)
        self.n_bias = {0: 4, 1: 2, 2: 10, 3: 2}[n]

    def alloc(self, sb):
        n = f"L{self.n}_"
        self.x, self.res = sb(n + "x", [P, T, D]), sb(n + "res", [P, T, D])
        self.adj = sb(n + "adj", [P, T, N])
        self.y = sb(n + "y", [P, T, D])
        self.stage = sb(n + "stage", [P, 2, KC, D])
        self.w_hi = sb(n + "w_hi", [P, len(self.mats), KC, D], F32R)
        self.w_lo = sb(n + "w_lo", [P, len(self.mats), KC, D], F32R)
        self.xT = sb(n + "xT", [P, 2, KC, N], F32R)
        self.stats, self.mv = sb(n + "stats", [P, QT, 6]), sb(n + "mv", [P, QT, 2])
        self.var, self.half = sb(n + "var", [P, QT]), sb(n + "half", [P, QT], I32)
        self.rstd, self.tmp = sb(n + "rstd", [P, QT]), sb(n + "tmp", [P, QT])
        if self.attn:
            self.edge = sb(n + "edge", [P, T, N])
            self.negmax, self.total = sb(n + "negmax", [P, NH, QT]), sb(n + "total", [P, NH, QT])
            self.rz = sb(n + "rz", [P, NH, QT])
            self.probs = sb(n + "probs", [P, NPB, QT, N])
            self.kq_parts = sb(n + "kq_parts", [P, 4, KC, N], F32R)
            self.kq_stack = sb(n + "kq_stack", [3 * HD, GP, J, 2, KC, N], F32R)
            self.v = sb(n + "v", [P, T, D])
            self.v_bias = sb(n + "v_bias", [P, D])
            self.shifted = sb(n + "shifted", [P, NSH, QT, N])
            self.pT = sb(n + "pT", [P, NPT, QT, N])
            self.oT = sb(n + "oT", [P, GROUPS, N])
            self.o = sb(n + "o", [P, QT, D])
            if self.proj:
                self.absmax = sb(n + "absmax", [P, NH, QT])
                self.fold = sb(n + "fold", [P, QT, N // 2])
                self.folded = sb(n + "folded", [P, FOLDS, QT, FOLDED])
                self.onT = sb(n + "onT", [P, QT, 2, KC, P], F32R)
                self.o_bias = sb(n + "o_bias", [P, D])
            else:
                self.neg_beta = sb(n + "neg_beta", [P, 1])
                self.kq_bias = sb(n + "kq_bias", [P, 2, KC])
        else:
            self.h = sb(n + "h", [P, T, D])
            self.hp = sb(n + "hp", [P, 3, T, D])
            self.rows = sb(n + "rows", [P, SUBS, 5, D])
            self.e, self.delta = sb(n + "e", [P, QT, N]), sb(n + "delta", [P, QT, N])
            self.dT = sb(n + "dT", [P, 6, P])
            self.rowmax, self.negmax = sb(n + "rowmax", [P, QT]), sb(n + "negmax", [P, QT])
            self.total, self.dsum = sb(n + "total", [P, QT]), sb(n + "dsum", [P, QT])
            self.diag, self.rdel = sb(n + "diag", [P, T]), sb(n + "rdel", [P, T])
            self.scr = sb(n + "scr", [P, P])
            self.c = sb(n + "c", [P, QT, D])

    def bias_loads(self, w):
        n = f"L{self.n}_gnn_"

        def row(name):
            return w[name].rearrange("(a d) -> a d", a=1).broadcast_to([P, D])
        if self.n == 0:
            yield self.neg_beta[:], w[n + "beta"].rearrange("(a d) -> a d", a=1).broadcast_to([P, 1])
            yield self.v_bias[:], row(n + "bv")
            for kq, name in enumerate(("bk", "bq")):
                yield self.kq_bias[:, kq, :], w[n + name]
        elif self.n == 2:
            for s in range(SUBS):
                for m, name in enumerate(("bl", "bs", "br", "ln_w", "ln_b")):
                    yield self.rows[:, s, m, :], w[n + name][s:s + 1, :].broadcast_to([P, D])
        else:
            yield self.v_bias[:], row(n + "bv")
            yield self.o_bias[:], row(n + "bo")


def halves(eng, half):
    half(-1, 1, False, False, True)
    half(0, 0, False, True, True)
    half(0, 1, True, True, True)
    with eng.Fori(1, PAIRS - 1) as i:
        half(i, 0, True, True, True)
        half(i, 1, True, True, True)
    half(PAIRS - 1, 0, True, True, True)
    half(PAIRS - 1, 1, True, True, False)
    half(PAIRS, 0, True, False, False)
    half(PAIRS, 1, False, False, False)


def units(eng, unit):
    for u in range(UNITS):
        unit(0, u, u > 0, True)
    with eng.Fori(1, PAIRS) as i:
        for u in range(UNITS):
            unit(i, u, True, True)
    unit(PAIRS, 0, True, False)


def is_graph(i, n):
    return not isinstance(i, int) or 0 <= GP * i + n < B


def head_at(i, b, s, lag, prev, cur):
    if s >= lag:
        return (b, s - lag) if cur else None
    return (b - 1, s - lag + H) if prev else None


def head_ahead(i, b, s, cur, nxt):
    if s < H - 1:
        return (b, s + 1) if cur else None
    return (b + 1, 0) if nxt else None


def build(nc, x_in, adj_in, w, out):
    ctx = ExitStack()
    with ctx:
        def sb(name, shape, dt=F32):
            return ctx.enter_context(nc.sbuf_tensor(name, shape, dt))

        sems = []

        def sem(name, credit=0):
            sems.append(Sem(ctx.enter_context(nc.semaphore(name)), credit))
            return sems[-1]

        def bank(name):
            return ctx.enter_context(nc.psum_tensor(name, [P, 512], F32))

        proj_ps = [bank(f"proj{r}") for r in range(2)]
        att_ps = [bank(f"att{r}") for r in range(2)]
        sc_ps = [bank(f"scores{r}") for r in range(2)]
        pt_ps = [bank(f"probsT{r}") for r in range(2)]

        ident = sb("ident", [P, P])
        before = sb("before", [P, P])
        behind = sb("behind", [P, P])

        init_done = sem("init_done")
        x_loaded = [sem(f"x_loaded{b}") for b in range(GP)]
        adj_loaded = [sem(f"adj_loaded{b}") for b in range(GP)]
        stored = [sem(f"stored{b}", 16) for b in range(GP)]
        w_loaded = [sem(f"w_loaded{m}") for m in range(2)]
        b_loaded = sem("b_loaded")
        stacked = [sem(f"stacked{j}") for j in range(J)]
        w_hi, w_lo = sem("w_hi"), sem("w_lo")
        pool_step = sem("pool_step")
        edge_step = sem("edge_step")
        newton_step = sem("newton_step")
        kept = sem("kept")
        edge_ready = sem("edge_ready")
        rstd_ready = sem("rstd_ready")
        proj_full = sem("proj_full")
        proj_hi = sem("proj_hi")
        proj_free = sem("proj_free", 2)
        proj_act = sem("proj_act", 2)
        heads_full = sem("heads_full")
        att_full = sem("att_full")
        oT_ready = sem("oT_ready")
        att_hi = sem("att_hi")
        att_free = sem("att_free", 2)
        sc_full = sem("sc_full")
        sc_read = sem("sc_read", 2)
        fold_half = sem("fold_half")
        fold_done = sem("fold_done", NSH)
        abs_done = sem("abs_done", 1)
        exp_done = sem("exp_done", NSH)
        ptp_full = sem("ptp_full", NPB)
        pt_act, pt_dve = sem("pt_act", 2), sem("pt_dve", 2)
        ln_step = sem("ln_step")
        y_ready = sem("y_ready", 2)
        red_done, max_ready = sem("red_done"), sem("max_ready")
        delta_ready = sem("delta_ready")
        d_step = sem("d_step")
        hp_ready = sem("hp_ready")

        xs = [x_in] + [nc.dram_tensor(f"x_after{n}", (B * N, D), F32, kind="Internal").ap()
                       for n in range(3)] + [out]
        adj_v = adj_in.rearrange("(n b) (q p) k -> b n p q k", b=GP, p=P)

        def nodes(ap):
            return ap.rearrange("(n b q p) d -> b n p q d", b=GP, q=QT, p=P)

        layers = [Layer(n) for n in range(4)]
        for L in layers:
            with ExitStack() as own:
                L.alloc(lambda name, shape, dt=F32: own.enter_context(nc.sbuf_tensor(name, shape, dt)))

        def enter(L):
            for b in range(GP):
                x_loaded[b].per = adj_loaded[b].per = stored[b].per = 16
            kept.per = y_ready.per = 1
            ln_step.per = L.steps
            if L.attn:
                for s in stacked:
                    s.per = 16 * 3
                proj_full.per, proj_hi.per = PROJ_USES, 3 * KC
                proj_free.per = PROJ_USES if L.proj else 3 * KC
                proj_act.per = 0 if L.proj else QT
                oT_ready.per = GROUPS
                att_free.per = (3 if L.proj else 1) * QT
                att_full.per = att_free.per
                heads_full.per = GROUPS
                att_hi.per = QT if L.proj else 0
                sc_full.per = sc_read.per = exp_done.per = ptp_full.per = H
                abs_done.per = H // 2 if L.proj else 0
                fold_half.per = fold_done.per = H if L.proj else 0
                edge_ready.per = rstd_ready.per = 1
                edge_step.per = 2 if L.n == 0 else 0
                newton_step.per = 4 * NEWTON
                pt_act.per, pt_dve.per = (H, 0) if L.proj else (H // 2, H // 2)
            else:
                proj_full.per, proj_hi.per, proj_free.per, proj_act.per = KC + 3 * QT, KC, KC, 3 * QT
                att_full.per = att_free.per = 1 + QT
                sc_full.per = exp_done.per = red_done.per = max_ready.per = delta_ready.per = QT
                d_step.per = 3 * QT
                hp_ready.per = 3 * QT

        def leave(L):
            for s in sems:
                s.base += s.per * PAIRS * (GP if L.attn else UNITS)
                s.per = 0
            for s in (*x_loaded, *adj_loaded, *stored):
                s.base -= 16 * PAIRS * ((GP if L.attn else UNITS) - 1)
            if not L.attn:
                for s in (kept, y_ready):
                    s.base -= PAIRS * (UNITS - GP)
            for m in range(2):
                w_loaded[m].base += 16 * len(L.mats[m::2])
            w_hi.base += len(L.mats)
            w_lo.base += len(L.mats)
            b_loaded.base += 16 * L.n_bias

        def heads_bank(L, n, gr):
            return att_ps[(ATT_USES[L.proj] * (n % GP) + HEADS_USE[L.proj][gr]) % 2]

        def end_bank(L, n, k):
            return att_ps[(ATT_USES[L.proj] * (n % GP) + END_USE[L.proj][k]) % 2]

        def begin():
            for s in sems:
                s.base, s.per = s.credit, 0

        block = ctx.enter_context(nc.Block())

        @block.sync
        def _(sp):
            begin()
            for b in range(GP):
                sp.sem_inc(stored[b].h, 16)
            for L in layers:
                enter(L)
                if L.n:
                    for b in range(GP):
                        sp.wait_ge(stored[b].h, stored[b].base)
                src_x, dst_x = nodes(xs[L.n]), nodes(xs[L.n + 1])

                def load(i, n):
                    b = n % GP
                    sp.dma_start(L.x[:, QT * b:QT * b + QT, :], src_x[b][i + n // GP]).then_inc(x_loaded[b].h, 16)
                    sp.dma_start(L.adj[:, QT * b:QT * b + QT, :], adj_v[b][i + n // GP]
                                 ).then_inc(adj_loaded[b].h, 16)

                def store(i, n):
                    b = n % GP
                    wait_apart(sp, y_ready, y_ready.at(graph(i, n), 1))
                    sp.dma_start(dst_x[b][i + n // GP], L.y[:, QT * b:QT * b + QT, :]).then_inc(stored[b].h, 16)

                load(0, 0)
                for m, name in enumerate(L.mats):
                    if m >= 2:
                        sp.wait_ge(w_lo.h, w_lo.base + m - 1)
                    sp.dma_start(L.stage[:, m % 2, :, :],
                                 w[name].rearrange("(c p) n -> p c n", p=P)).then_inc(w_loaded[m % 2].h, 16)
                    if m == 0:
                        for dst, src in L.bias_loads(w):
                            sp.dma_start(dst, src).then_inc(b_loaded.h, 16)
                load(0, 1)

                def half(i, b, prev, cur, nxt):
                    if is_graph(i, b) and is_graph(i, b + GP):
                        wait_apart(sp, kept, kept.at(graph(i, b), 1))
                        wait_apart(sp, edge_ready, edge_ready.at(graph(i, b), 1))
                        wait_apart(sp, proj_full, proj_full.at(graph(i, b), KC))
                        load(i, b + GP)
                    if nxt:
                        g, nb = graph(i, b + 1), (b + 1) % GP
                        wait_apart(sp, proj_free, proj_free.at(g, V_USE))
                        for j in range(J):
                            for r, (first, step) in enumerate(((0, 2), (0, 3), (1, 1))):
                                sp.dma_start(L.kq_stack[HD * r:HD * r + HD, nb, j, :, :, :].bitcast(F32),
                                             L.kq_parts[HD * j:HD * j + HD, first:first + step + 1:step, :, :]
                                             .bitcast(F32)).then_inc(stacked[j].h, 16)
                    if is_graph(i, b - 2):
                        store(i, b - 2)

                def unit(i, u, prev, cur):
                    s, b = divmod(u, GP)
                    if cur and s == 1 and not (isinstance(i, int) and i == PAIRS - 1):
                        wait_apart(sp, kept, kept.at(graph(i, b), 1))
                        wait_apart(sp, proj_full, proj_full.at(stage_unit(i, b), KC))
                        wait_apart(sp, delta_ready, delta_ready.at(stage_unit(i, u), QT))
                        load(i, b + GP)
                    if prev and u in (0, 3):
                        store(i, -1 if u == 0 else 0)

                if L.attn:
                    halves(sp, half)
                else:
                    for u in range(UNITS):
                        unit(0, u, u > 0, True)
                    with sp.Fori(1, PAIRS - 1) as i:
                        for u in range(UNITS):
                            unit(i, u, True, True)
                    for u in range(UNITS):
                        unit(PAIRS - 1, u, True, True)
                    unit(PAIRS, 0, True, False)
                leave(L)
            for b in range(GP):
                sp.wait_ge(stored[b].h, stored[b].base)

        @block.gpsimd
        def _(pool):
            begin()
            g_ = nc.gpsimd
            pool.sem_inc(fold_done.h, NSH)
            g_.memset(ident[:], 0.0).then_inc(pool_step.h, 1)
            g_.memset(before[:], 1.0).then_inc(pool_step.h, 1)
            g_.memset(behind[:], 1.0).then_inc(pool_step.h, 1)
            pool.wait_ge(pool_step.h, 3)
            g_.affine_select(out=ident[:], in_=ident[:], compare_op=ALU.not_equal, fill=1.0, base=0,
                             pattern=[[-1, P]], channel_multiplier=1).then_inc(init_done.h, 1)
            g_.affine_select(out=before[:], in_=before[:], compare_op=ALU.is_gt, fill=0.0, base=0,
                             pattern=[[1, P]], channel_multiplier=-1).then_inc(init_done.h, 1)
            g_.affine_select(out=behind[:], in_=behind[:], compare_op=ALU.is_gt, fill=0.0, base=0,
                             pattern=[[-1, P]], channel_multiplier=1).then_inc(init_done.h, 1)
            def keep_residual(L, i, n, prev=False):
                g, b = graph(i, n), n % GP
                pool.wait_ge(x_loaded[b].h, x_loaded[b].at(of_parity(i, n), 16))
                if not L.attn:
                    wait_apart(pool, y_ready, y_ready.at(g, -1))
                    tiles = slice(QT * b, QT * b + QT)
                    g_.tensor_copy(L.res[:, tiles, :], L.x[:, tiles, :]).then_inc(kept.h, 1)
                    return
                if prev:
                    if L.proj:
                        pool.wait_ge(att_free.h, att_free.at(graph(i, n - 2), 3 * QT))
                    else:
                        pool.wait_ge(ln_step.h, ln_step.at(graph(i, n - 2), L.steps - ESTIMATE - 2))
                row = L.o_bias if L.proj else L.v_bias
                for t in range(QT * b, QT * b + QT):
                    ins = g_.tensor_tensor(L.res[:, t, :], L.x[:, t, :], row[:], ALU.add)
                ins.then_inc(kept.h, 1)

            def keep_edge(L, i, n, prev):
                g, b = graph(i, n), n % GP
                tiles = slice(QT * b, QT * b + QT)
                if prev:
                    pool.wait_ge(sc_read.h, sc_read.at(g, -H))
                wait_apart(pool, adj_loaded[b], adj_loaded[b].at(of_parity(i, n), 16))
                if L.n == 0:
                    g_.tensor_scalar(L.edge[:, tiles, :], L.adj[:, tiles, :], 0.0, MASKED, ALU.is_le, ALU.mult
                                     ).then_inc(edge_step.h, 1)
                    g_.tensor_scalar(L.adj[:, tiles, :], L.adj[:, tiles, :], L.neg_beta[:], None, ALU.mult
                                     ).then_inc(edge_step.h, 1)
                    pool.wait_ge(edge_step.h, edge_step.at(g, 2))
                    g_.tensor_tensor(L.edge[:, tiles, :], L.edge[:, tiles, :], L.adj[:, tiles, :], ALU.add
                                     ).then_inc(edge_ready.h, 1)
                else:
                    g_.tensor_scalar(L.edge[:, tiles, :], L.adj[:, tiles, :], -1.0 if L.n == 1 else -2.0,
                                     None, ALU.mult).then_inc(edge_ready.h, 1)

            def newton(L, g):
                pool.wait_ge(ln_step.h, ln_step.at(g, L.steps))
                for step in range(0, 4 * NEWTON, 4):
                    g_.tensor_tensor(L.tmp[:], L.rstd[:], L.rstd[:], ALU.mult).then_inc(newton_step.h, 1)
                    pool.wait_ge(newton_step.h, newton_step.at(g, step + 1))
                    g_.tensor_tensor(L.tmp[:], L.tmp[:], L.var[:], ALU.mult).then_inc(newton_step.h, 1)
                    wait_apart(pool, newton_step, newton_step.at(g, step + 2))
                    g_.tensor_scalar(L.tmp[:], L.tmp[:], -0.5, 1.5, ALU.mult, ALU.add).then_inc(newton_step.h, 1)
                    pool.wait_ge(newton_step.h, newton_step.at(g, step + 3))
                    g_.tensor_tensor(L.rstd[:], L.rstd[:], L.tmp[:], ALU.mult).then_inc(newton_step.h, 1)
                    pool.wait_ge(newton_step.h, newton_step.at(g, step + 4))
                pool.sem_inc(rstd_ready.h, 1)

            def half(L, i, b, prev, cur, nxt):
                for s in range(H):
                    at = head_ahead(i, b, s, cur, nxt)
                    if at and L.proj:
                        g, h = graph(i, at[0]), at[1]
                        pool.wait_ge(fold_done.h, fold_done.at(g, h))
                        pool.wait_ge(sc_read.h, sc_read.at(g, h + 1))
                        g_.tensor_tensor(L.fold[:], L.shifted[:, h % NSH, :, 0:N // 2],
                                         L.shifted[:, h % NSH, :, N // 2:N], ALU.add).then_inc(fold_half.h, 1)
                        pool.wait_ge(abs_done.h, abs_done.at(g, h // 2 + 1 - FOLDS // 2))
                        pool.wait_ge(fold_half.h, fold_half.at(g, h + 1))
                        g_.tensor_tensor(L.folded[:, h % FOLDS, :, :], L.fold[:, :, 0:FOLDED],
                                         L.fold[:, :, FOLDED:2 * FOLDED], ALU.add).then_inc(fold_done.h, 1)
                    if nxt and s == KEEP_EDGE:
                        keep_edge(L, i, b + 1, prev)
                    if cur and s == KEEP_RES:
                        keep_residual(L, i, b, is_graph(i, b - 2))
                    if is_graph(i, b - 2) and s == ESTIMATED:
                        newton(L, graph(i, b - 2))

            for L in layers:
                enter(L)
                pool.wait_ge(b_loaded.h, b_loaded.base + 16 * L.n_bias)
                if L.n == 0:
                    g_.tensor_scalar(L.neg_beta[:], L.neg_beta[:], -1.0, None, ALU.mult).then_inc(pool_step.h, 1)
                    pool.wait_ge(pool_step.h, 4)
                if L.attn:
                    halves(pool, lambda *a: half(L, *a))
                else:
                    with pool.Fori(0, PAIRS) as i:
                        for u in range(UNITS):
                            s, b = divmod(u, GP)
                            for q in range(QT):
                                for m in range(3):
                                    n = 3 * q + m + 1
                                    pool.wait_ge(proj_act.h, proj_act.at(stage_unit(i, u), n))
                                    hp = L.hp[:, m, QT * b + q, :]
                                    g_.tensor_tensor(hp, hp, L.rows[:, s, m, :], ALU.add).then_inc(hp_ready.h, 1)
                            if s == 0:
                                keep_residual(L, i, b)
                leave(L)

        @block.tensor
        def _(pe):
            begin()
            pe.sem_inc(ptp_full.h, NPB)
            pe.wait_ge(init_done.h, 3)
            t_ = nc.tensor

            def parts3(ps, lhsT, rhs):
                terms = [(c, a, b) for c in range(KC) for a, b in ((0, 0), (0, 1), (1, 0))]
                for n, (c, a, b) in enumerate(terms):
                    mm = t_.matmul(ps, lhsT(a, c), rhs(b, c), start=n == 0, stop=n == len(terms) - 1)
                return mm

            for L in layers:
                enter(L)

                def w_part(m):
                    return lambda a, c: (L.w_hi, L.w_lo)[a][:, m, c, :]

                def transpose_chunk(ps, src, b, c):
                    for q in range(QT):
                        mm = t_.transpose(ps[:, P * q:P * q + P], src[:, QT * b + q, P * c:P * c + P], ident[:])
                    return mm

                def project(i, n, u):
                    g, b = graph(i, n), n % GP
                    ps = proj_ps[(PROJ_USES * b + u) % 2]
                    free = proj_free if L.proj or u >= 2 else proj_act
                    pe.wait_ge(free.h, free.at(g, u - 1))
                    if u == 0:
                        pe.wait_ge(x_loaded[b].h, x_loaded[b].at(of_parity(i, n), 16))
                    if u < K_USE:
                        mm = transpose_chunk(ps, L.x, b, u)
                    elif u < V_USE:
                        if u == K_USE:
                            pe.wait_ge(proj_free.h, proj_free.at(g, KC))
                        m, c = divmod(u - K_USE, KC)
                        mm = parts3(ps[:, 0:N], lambda a, k: w_part(m)(a, k)[:, P * c:P * c + P],
                                    lambda a, k: L.xT[:, a, k, :])
                    else:
                        q = u - V_USE
                        mm = parts3(ps[:, 0:D], lambda a, k: L.xT[:, a, k, P * q:P * q + P], w_part(2))
                    mm.then_inc(proj_full.h, 1)

                def scores(g, b, h):
                    j, c = divmod(h, KC)
                    if c == 0:
                        pe.wait_ge(stacked[j].h, stacked[j].at(g, 16 * 3))
                    pe.wait_ge(sc_read.h, sc_read.at(g, h + 1 - 2))
                    for q in range(QT):
                        mm = t_.matmul(sc_ps[h % 2][:, N * q:N * q + N],
                                       L.kq_stack[:, b, j, 1, c, P * q:P * q + P],
                                       L.kq_stack[:, b, j, 0, c, :], start=True, stop=True)
                    mm.then_inc(sc_full.h, 1)

                def half(i, b, prev, cur, nxt):
                    for s in range(H):
                        at = head_ahead(i, b, s, cur, nxt)
                        if at:
                            scores(graph(i, at[0]), at[0] % GP, at[1])
                        at = head_at(i, b, s, LAG_T, prev, cur)
                        if at:
                            n, h = at
                            g = graph(i, n)
                            pe.wait_ge(exp_done.h, exp_done.at(g, h + 1))
                            if L.proj:
                                pe.wait_ge(pt_act.h, pt_act.at(g, h - 1))
                            else:
                                ev = (pt_act, pt_dve)[h % 2]
                                pe.wait_ge(ev.h, ev.at(g, h // 2))
                            for kt in range(QT):
                                for q in range(QT):
                                    mm = t_.transpose(pt_ps[h % 2][:, N * kt + P * q:N * kt + P * q + P],
                                                      L.probs[:, h % NPB, q, P * kt:P * kt + P], ident[:])
                            mm.then_inc(ptp_full.h, 1)
                        at = head_at(i, b, s, LAG_PV, prev, cur)
                        if at and at[1] % J == J - 1:
                            n, h = at
                            g, nb, gr = graph(i, n), n % GP, h // J
                            if L.proj:
                                pe.wait_ge(pt_act.h, pt_act.at(g, h + 1))
                            else:
                                pe.wait_ge(pt_act.h, pt_act.at(g, h // 2 + 1))
                                pe.wait_ge(pt_dve.h, pt_dve.at(g, h // 2 + 1))
                            if gr == 0:
                                if L.proj:
                                    pe.wait_ge(proj_free.h, proj_free.at(g, PROJ_USES))
                                else:
                                    pe.wait_ge(proj_act.h, proj_act.at(g, QT))
                            if gr == GROUPS - 1 and not L.proj:
                                pe.wait_ge(oT_ready.h, oT_ready.at(g, 1))
                            elif gr == GROUPS - 1:
                                if is_graph(i, n - 1):
                                    pe.wait_ge(att_free.h, att_free.at(graph(i, n - 1), 2 * QT + 1))
                            elif is_graph(i, n - 1):
                                pe.wait_ge(att_free.h, att_free.at(graph(i, n - 1), 1 + gr * (QT if L.proj else 1)))
                            ps = heads_bank(L, n, gr)
                            for kt in range(QT):
                                for k in range(J):
                                    hh = J * gr + k
                                    mm = t_.matmul(ps[HD * k:HD * k + HD, 0:N],
                                                   L.v[:, QT * nb + kt, HD * hh:HD * hh + HD],
                                                   L.pT[:, (H * nb + hh) % NPT, kt, :],
                                                   start=kt == 0, stop=kt == QT - 1)
                            mm.then_inc(heads_full.h, 1)
                        if prev and s == NAT:
                            pe.wait_ge(oT_ready.h, oT_ready.at(graph(i, b - 1), GROUPS))
                            if L.proj and is_graph(i, b - 2):
                                pe.wait_ge(att_free.h, att_free.at(graph(i, b - 2), 3 * QT))
                            for q in range(QT):
                                ps = end_bank(L, b - 1, q)
                                for gr in range(GROUPS):
                                    mm = t_.transpose(ps[:, P * gr:P * gr + P], L.oT[:, gr, P * q:P * q + P], ident[:])
                                mm.then_inc(att_full.h, 1)
                        if prev and L.proj and s == ONT:
                            pe.wait_ge(att_free.h, att_free.at(graph(i, b - 1), QT))
                            for q in range(QT):
                                ps = end_bank(L, b - 1, QT + q)
                                if cur and q == 1:
                                    pe.wait_ge(oT_ready.h, oT_ready.at(graph(i, b), 1))
                                for c in range(KC):
                                    mm = t_.transpose(ps[:, P * c:P * c + P], L.o[:, q, P * c:P * c + P], ident[:])
                                mm.then_inc(att_full.h, 1)
                        if is_graph(i, b - 2) and L.proj and OUT <= s < OUT + QT:
                            q = s - OUT
                            pe.wait_ge(att_free.h, att_free.at(graph(i, b - 2), 2 * QT))
                            if prev and q == 1:
                                pe.wait_ge(oT_ready.h, oT_ready.at(graph(i, b - 1), 2))
                            parts3(end_bank(L, b - 2, 2 * QT + q)[:, 0:D], lambda a, k: L.onT[:, q, a, k, :],
                                   w_part(3)).then_inc(att_full.h, 1)
                        if nxt:
                            for u in PROJ_AT.get(s, ()):
                                project(i, b + 1, u)

                def unit(i, u, prev, cur):
                    s, b = divmod(u % UNITS, GP)
                    g = stage_unit(i, u)
                    p_bank = proj_full.per * u
                    if cur:
                        if s == 0:
                            pe.wait_ge(x_loaded[b].h, x_loaded[b].at(of_parity(i, b), 16))
                        else:
                            pe.wait_ge(ln_step.h, ln_step.at(stage_unit(i, u - GP), L.steps))
                        for c in range(KC):
                            free, k = (proj_act, c - 1) if c < 2 else (proj_free, c - 1)
                            pe.wait_ge(free.h, free.at(g, k))
                            transpose_chunk(proj_ps[(p_bank + c) % 2], L.h if s else L.x, b, c
                                            ).then_inc(proj_full.h, 1)
                        pe.wait_ge(proj_free.h, proj_free.at(g, KC))
                        for q in range(QT):
                            pe.wait_ge(exp_done.h, exp_done.at(g, q + 1 - 2))
                            parts3(sc_ps[q][:, 0:N], lambda a, k: L.xT[:, a, k, P * q:P * q + P],
                                   lambda a, k: L.xT[:, a, k, :]).then_inc(sc_full.h, 1)
                    if prev:
                        gp, pb = stage_unit(i, u - 1), (u - 1) % GP
                        pe.wait_ge(hp_ready.h, hp_ready.at(gp, 3 * QT))
                        pe.wait_ge(att_free.h, att_free.at(gp, 1))
                        for it in range(QT):
                            ps = att_ps[(3 * (u - 1) + 1 + it) % 2]
                            for n, (blk, m, jt) in enumerate([((0, 0, 0), (1, 0, 1), (3, 2, 0)),
                                                              ((2, 0, 1), (4, 2, 0), (5, 2, 1))][it]):
                                mm = t_.matmul(ps[:, 0:D], L.dT[:, blk, :], L.hp[:, m, QT * pb + jt, :],
                                               start=n == 0, stop=n == 2)
                            mm.then_inc(att_full.h, 1)
                    if cur:
                        for q in range(QT):
                            for m in range(3):
                                n = 3 * q + m
                                free, k = (proj_free, KC - 1 + n) if n < 2 else (proj_act, n - 1)
                                pe.wait_ge(free.h, free.at(g, k))
                                parts3(proj_ps[(p_bank + KC + n) % 2][:, 0:D],
                                       lambda a, k: L.xT[:, a, k, P * q:P * q + P], w_part(3 * s + m)
                                       ).then_inc(proj_full.h, 1)
                        pe.wait_ge(delta_ready.h, delta_ready.at(g, QT))
                        pe.wait_ge(att_free.h, att_free.at(g, -1))
                        for jt in range(QT):
                            for it in range(QT):
                                mm = t_.transpose(att_ps[3 * u % 2][:, N * jt + P * it:N * jt + P * it + P],
                                                  L.delta[:, it, P * jt:P * jt + P], ident[:])
                        mm.then_inc(att_full.h, 1)

                pe.wait_ge(w_lo.h, w_lo.base + len(L.mats))
                if L.attn:
                    halves(pe, half)
                else:
                    units(pe, unit)
                leave(L)

        @block.scalar
        def _(act):
            begin()
            act.sem_inc(exp_done.h, NSH)
            act.sem_inc(pt_act.h, 2)
            act.sem_inc(proj_act.h, 2)
            a_ = nc.scalar
            for L in layers:
                enter(L)
                for m in range(len(L.mats)):
                    act.wait_ge(w_loaded[m % 2].h, w_loaded[m % 2].base + 16 * (m // 2 + 1))
                    kq = L.attn and m < 2
                    f = -L.scale if L.attn and m == 1 else 1.0
                    for c in range(KC):
                        src, dst = L.stage[:, m % 2, c, :], L.w_hi[:, m, c, :]
                        if kq:
                            for k in range(KC):
                                ins = a_.activation(dst[:, P * k:P * k + P].rearrange("p (j d) -> p j d", j=J),
                                                    src.rearrange("p (j c d) -> p c j d", j=J, c=KC)[:, k],
                                                    ACT.Copy, scale=f)
                        else:
                            ins = a_.activation(dst, src, ACT.Copy, scale=f)
                    ins.then_inc(w_hi.h, 1)
                if L.n == 0:
                    act.wait_ge(b_loaded.h, b_loaded.base + 16 * L.n_bias)
                    act.wait_ge(w_lo.h, w_lo.base + len(L.mats))

                def project(i, n, u):
                    g, b = graph(i, n), n % GP
                    ps = proj_ps[(PROJ_USES * b + u) % 2]
                    if u >= V_USE and L.proj:
                        return
                    act.wait_ge(proj_full.h, proj_full.at(g, u + 1))
                    if u >= V_USE:
                        a_.activation(L.v[:, QT * b + u - V_USE, :], ps[:, 0:D], ACT.Copy).then_inc(proj_act.h, 1)
                    elif u < K_USE:
                        a_.activation(L.xT[:, 0, u, :], ps[:, 0:N], ACT.Copy).then_inc(proj_hi.h, 1)
                    else:
                        m, c = divmod(u - K_USE, KC)
                        if u == K_USE:
                            for j in range(J):
                                act.wait_ge(stacked[j].h, stacked[j].at(g, 0))
                        if L.n == 0:
                            a_.activation(L.kq_parts[:, 2 * m, c, :], ps[:, 0:N], ACT.Identity,
                                          bias=L.kq_bias[:, m, c:c + 1]).then_inc(proj_hi.h, 1)
                        else:
                            a_.activation(L.kq_parts[:, 2 * m, c, :], ps[:, 0:N], ACT.Copy).then_inc(proj_hi.h, 1)

                def half(i, b, prev, cur, nxt):
                    for s in range(H):
                        if nxt:
                            for u in PROJ_AT.get(s - 1, ()):
                                project(i, b + 1, u)
                        if cur:
                            g = graph(i, b)
                            act.wait_ge(sc_read.h, sc_read.at(g, s + 1))
                            act.wait_ge(ptp_full.h, ptp_full.at(g, s + 1 - NPB))
                            for q in range(QT):
                                ins = a_.activation(L.probs[:, s % NPB, q, :], L.shifted[:, s % NSH, q, :],
                                                    ACT.Exp, scale=-1.0, bias=L.negmax[:, H * b + s, q:q + 1],
                                                    accum_out=L.total[:, H * b + s, q:q + 1])
                            ins.then_inc(exp_done.h, 1)
                        if prev and L.proj and s == ONT + 1:
                            for q in range(QT):
                                u = QT + q
                                act.wait_ge(att_full.h, att_full.at(graph(i, b - 1), u + 1))
                                a_.activation(L.onT[:, q, 0, :, :].rearrange("p c n -> p (c n)"),
                                              end_bank(L, b - 1, u)[:, 0:D], ACT.Copy
                                              ).then_inc(att_hi.h, 1)
                        at = head_at(i, b, s, LAG_T, prev, cur)
                        if at and (L.proj or at[1] % 2 == 0):
                            n, h = at
                            act.wait_ge(ptp_full.h, ptp_full.at(graph(i, n), h + 1))
                            a_.activation(L.pT[:, (H * (n % GP) + h) % NPT, :, :].rearrange("p k n -> p (k n)"),
                                          pt_ps[h % 2][:], ACT.Copy).then_inc(pt_act.h, 1)
                        at = head_at(i, b, s, LAG_PV, prev, cur)
                        if at and at[1] % J == J - 1:
                            n, gr = at[0], at[1] // J
                            act.wait_ge(heads_full.h, heads_full.at(graph(i, n), gr + 1))
                            a_.activation(L.oT[:, gr, :], heads_bank(L, n, gr)[:, 0:N],
                                          ACT.Copy).then_inc(oT_ready.h, 1)

                def unit(i, u, prev, cur):
                    if not cur:
                        return
                    g, b = stage_unit(i, u), u % GP
                    p_bank = proj_full.per * u
                    for c in range(KC):
                        act.wait_ge(proj_full.h, proj_full.at(g, c + 1))
                        a_.activation(L.xT[:, 0, c, :], proj_ps[(p_bank + c) % 2][:, 0:N], ACT.Copy
                                      ).then_inc(proj_hi.h, 1)
                    for q in range(QT):
                        act.wait_ge(max_ready.h, max_ready.at(g, q + 1))
                        a_.activation(L.e[:, q, :], sc_ps[q][:, 0:N], ACT.Exp, scale=L.scale,
                                      bias=L.negmax[:, q:q + 1], accum_out=L.total[:, q:q + 1]
                                      ).then_inc(exp_done.h, 1)
                    if not (isinstance(i, int) and i == 0 and u < GP):
                        act.wait_ge(att_free.h, att_free.at(stage_unit(i, u - GP), 1 + QT))
                    for q in range(QT):
                        for m in range(3):
                            n = KC + 3 * q + m
                            act.wait_ge(proj_full.h, proj_full.at(g, n + 1))
                            a_.activation(L.hp[:, m, QT * b + q, :], proj_ps[(p_bank + n) % 2][:, 0:D], ACT.Copy
                                          ).then_inc(proj_act.h, 1)

                if L.attn:
                    halves(act, half)
                else:
                    units(act, unit)
                leave(L)

        @block.vector
        def _(dve):
            begin()
            dve.sem_inc(proj_free.h, 2)
            dve.sem_inc(att_free.h, 2)
            dve.sem_inc(sc_read.h, 2)
            dve.sem_inc(pt_dve.h, 2)
            dve.sem_inc(y_ready.h, 2)
            dve.sem_inc(abs_done.h, 1)
            v_ = nc.vector
            dve.wait_ge(init_done.h, 3)
            for L in layers:
                enter(L)
                for m in range(len(L.mats)):
                    dve.wait_ge(w_hi.h, w_hi.base + m + 1)
                    kq = L.attn and m < 2
                    f = -L.scale if L.attn and m == 1 else 1.0
                    if L.n == 0 and m == 1:
                        dve.wait_ge(b_loaded.h, b_loaded.base + 16 * L.n_bias)
                        v_.tensor_scalar(L.kq_bias[:, 1, :], L.kq_bias[:, 1, :], f, None, ALU.mult)
                    for c in range(KC):
                        src, hi, dst = L.stage[:, m % 2, c, :], L.w_hi[:, m, c, :], L.w_lo[:, m, c, :]
                        if kq:
                            for k in range(KC):
                                sl = slice(P * k, P * k + P)
                                ins = v_.scalar_tensor_tensor(
                                    out=dst[:, sl].rearrange("p (j d) -> p j d", j=J),
                                    in0=src.rearrange("p (j c d) -> p c j d", j=J, c=KC)[:, k], scalar=f,
                                    in1=hi[:, sl].bitcast(F32).rearrange("p (j d) -> p j d", j=J),
                                    op0=ALU.mult, op1=ALU.subtract)
                        else:
                            ins = v_.scalar_tensor_tensor(out=dst, in0=src, scalar=f, in1=hi.bitcast(F32),
                                                          op0=ALU.mult, op1=ALU.subtract)
                    ins.then_inc(w_lo.h, 1)
                dve.wait_ge(b_loaded.h, b_loaded.base + 16 * L.n_bias)
                dve.wait_ge(w_lo.h, w_lo.base + len(L.mats))

                class Chain:

                    def __init__(self, unit, n=0):
                        self.unit, self.n = unit, n

                    def step(self, ins, wait=True, more=0):
                        self.n += 1 + more
                        ins.then_inc(ln_step.h, 1 + more)
                        if wait:
                            self.wait()

                    def wait(self):
                        wait_apart(dve, ln_step, ln_step.at(self.unit, self.n))

                    def estimate(self, eps):
                        self.wait()
                        self.step(v_.tensor_scalar(L.var[:], L.mv[:, :, 1], eps, None, ALU.add))
                        self.step(v_.tensor_scalar(L.half[:], L.var[:].bitcast(I32), 1, None,
                                                   ALU.logical_shift_right))
                        self.step(v_.tensor_scalar(L.rstd[:].bitcast(I32), L.half[:], -1.0, RSQRT_MAGIC,
                                                   ALU.mult, ALU.add))

                    def newton(self):
                        for _ in range(NEWTON):
                            self.step(v_.scalar_tensor_tensor(out=L.tmp[:], in0=L.rstd[:], scalar=-0.5,
                                                              in1=L.rstd[:], op0=ALU.mult, op1=ALU.mult))
                            self.step(v_.tensor_tensor(L.tmp[:], L.tmp[:], L.var[:], ALU.mult))
                            self.step(v_.scalar_tensor_tensor(out=L.rstd[:], in0=L.tmp[:], scalar=1.5,
                                                              in1=L.rstd[:], op0=ALU.add, op1=ALU.mult))

                    def statistics(self, tiles, eps):
                        for q, tile in enumerate(tiles):
                            self.step(v_.bn_stats(L.stats[:, q, :], tile), wait=q == QT - 1)
                        for q in range(QT):
                            self.step(v_.bn_aggr(L.mv[:, q, :], L.stats[:, q, :]), wait=q == QT - 1)
                        self.estimate(eps)

                    def statistics_of(self, q, tile):
                        self.wait()
                        self.step(v_.bn_stats(L.stats[:, q, :], tile))
                        self.step(v_.bn_aggr(L.mv[:, q, :], L.stats[:, q, :]), wait=False)

                    def layer_norm(self, b):
                        self.statistics([L.y[:, QT * b + q, :] for q in range(QT)], LN_EPS)
                        self.newton()
                        assert self.n == L.steps, (L.n, self.n, L.steps)
                        apply(b)

                def apply(b):
                    for q in range(QT):
                        tile = L.y[:, QT * b + q, :]
                        ins = v_.tensor_scalar(tile, tile, L.mv[:, q, 0:1], L.rstd[:, q:q + 1],
                                               ALU.subtract, ALU.mult)
                    ins.then_inc(y_ready.h, 1)

                def y_free(i, n):
                    dve.wait_ge(stored[n % GP].h, stored[n % GP].at(of_parity(i, n), 0))

                def low(dst, ps, hi, bias=None):
                    hi = hi.bitcast(F32)
                    if bias is None:
                        return v_.tensor_tensor(dst, ps, hi, ALU.subtract)
                    return v_.scalar_tensor_tensor(out=dst, in0=ps, scalar=bias, in1=hi,
                                                   op0=ALU.add, op1=ALU.subtract)

                def project(i, n, u):
                    g, b = graph(i, n), n % GP
                    ps = proj_ps[(PROJ_USES * b + u) % 2]
                    if u >= V_USE:
                        if L.proj:
                            dve.wait_ge(proj_full.h, proj_full.at(g, u + 1))
                            v_.tensor_tensor(L.v[:, QT * b + u - V_USE, :], ps[:, 0:D], L.v_bias[:], ALU.add
                                             ).then_inc(proj_free.h, 1)
                        return
                    dve.wait_ge(proj_hi.h, proj_hi.at(g, u + 1))
                    if u < K_USE:
                        ins = low(L.xT[:, 1, u, :], ps[:, 0:N], L.xT[:, 0, u, :])
                    else:
                        m, c = divmod(u - K_USE, KC)
                        ins = low(L.kq_parts[:, 2 * m + 1, c, :], ps[:, 0:N], L.kq_parts[:, 2 * m, c, :],
                                  L.kq_bias[:, m, c:c + 1] if L.n == 0 else None)
                    ins.then_inc(proj_free.h, 1)

                def half(i, b, prev, cur, nxt):
                    gp, pb = graph(i, b - 1), (b - 1) % GP
                    gpp, ppb = graph(i, b - 2), b % GP
                    if prev:
                        chain = Chain(gp)
                    if is_graph(i, b - 2):
                        ending = Chain(gpp, 3 if L.proj else 1)
                    for s in range(H):
                        at = head_ahead(i, b, s, cur, nxt)
                        if at:
                            n, h = at
                            g = graph(i, n)
                            if h == 0:
                                dve.wait_ge(edge_ready.h, edge_ready.at(g, 1))
                            dve.wait_ge(sc_full.h, sc_full.at(g, h + 1))
                            wait_apart(dve, exp_done, exp_done.at(g, h + 1 - NSH))
                            if L.proj:
                                wait_apart(dve, fold_done, fold_done.at(g, h + 1 - NSH))
                            for q in range(QT):
                                ins = v_.tensor_tensor_reduce(
                                    L.shifted[:, h % NSH, q, :], sc_ps[h % 2][:, N * q:N * q + N],
                                    L.edge[:, QT * (n % GP) + q, :], 1.0, FMAX, ALU.add, ALU.min,
                                    L.negmax[:, H * (n % GP) + h, q:q + 1])
                            ins.then_inc(sc_read.h, 1)
                        if nxt:
                            for u in PROJ_AT.get(s - 1, ()):
                                project(i, b + 1, u)
                        at = head_at(i, b, s, 2, prev, cur)
                        if at and L.proj and at[1] % 2 == 1:
                            n, h = at
                            hb = H * (n % GP) + h
                            wait_apart(dve, fold_done, fold_done.at(graph(i, n), h + 1))
                            v_.tensor_reduce(L.absmax[:, hb - 1:hb + 1, :],
                                             L.folded[:, h % FOLDS - 1:h % FOLDS + 1, :, :], AX.X, ALU.max
                                             ).then_inc(abs_done.h, 1)
                        if is_graph(i, b - 2) and SUM < s <= SUM + QT:
                            q = s - 1 - SUM
                            if L.proj:
                                dve.wait_ge(att_free.h, att_free.at(gpp, 2 * QT + q + 1))
                            ending.statistics_of(q, L.y[:, QT * ppb + q, :])
                        if is_graph(i, b - 2) and SUM <= s < SUM + QT:
                            q = s - SUM
                            t = QT * ppb + q
                            if q == 0:
                                y_free(i, b - 2)
                                dve.wait_ge(kept.h, kept.at(gpp, 1))
                            if L.proj:
                                dve.wait_ge(att_full.h, att_full.at(gpp, 2 * QT + q + 1))
                                v_.tensor_tensor(L.y[:, t, :], end_bank(L, b - 2, 2 * QT + q)[:, 0:D],
                                                 L.res[:, t, :], ALU.add).then_inc(att_free.h, 1)
                            else:
                                dve.wait_ge(att_free.h, att_free.at(gpp, q + 1))
                                ending.step(v_.tensor_tensor(L.y[:, t, :], L.o[:, q, :], L.res[:, t, :], ALU.add),
                                            wait=False)
                        if is_graph(i, b - 2) and s == ESTIMATED:
                            ending.estimate(LN_EPS)
                            assert ending.n == L.steps
                        if is_graph(i, b - 2) and s == APPLY:
                            wait_apart(dve, rstd_ready, rstd_ready.at(gpp, 1))
                            apply(ppb)
                        if prev and s == NAT:
                            hs = slice(H * pb, H * pb + H)
                            dve.wait_ge(exp_done.h, exp_done.at(gp, H))
                            chain.step(v_.reciprocal(L.rz[:, hs, :], L.total[:, hs, :]), wait=False)
                            if L.proj:
                                dve.wait_ge(abs_done.h, abs_done.at(gp, H // 2))
                                chain.step(v_.scalar_tensor_tensor(
                                    out=L.absmax[:, hs, :], in0=L.negmax[:, hs, :], scalar=0.0,
                                    in1=L.absmax[:, hs, :], op0=ALU.not_equal, op1=ALU.max))
                                chain.step(v_.scalar_tensor_tensor(
                                    out=L.rz[:, hs, :], in0=L.absmax[:, hs, :], scalar=0.0,
                                    in1=L.rz[:, hs, :], op0=ALU.is_gt, op1=ALU.mult), wait=False)
                        if prev and s == NAT + 1:
                            chain.wait()
                            hs = slice(H * pb, H * pb + H)
                            for q in range(QT):
                                dve.wait_ge(att_full.h, att_full.at(gp, q + 1))
                                v_.tensor_tensor(
                                    L.o[:, q, :].rearrange("p (h d) -> p h d", h=H),
                                    end_bank(L, b - 1, q)[:, 0:D].rearrange("p (h d) -> p h d", h=H),
                                    L.rz[:, hs, q:q + 1].broadcast_to([P, H, HD]), ALU.mult
                                ).then_inc(att_free.h, 1)
                        if prev and L.proj and s == ONT + 1:
                            for q in range(QT):
                                dve.wait_ge(att_hi.h, att_hi.at(gp, q + 1))
                                low(L.onT[:, q, 1, :, :].rearrange("p c n -> p (c n)"),
                                    end_bank(L, b - 1, QT + q)[:, 0:D],
                                    L.onT[:, q, 0, :, :].rearrange("p c n -> p (c n)")).then_inc(att_free.h, 1)
                        at = head_at(i, b, s, LAG_T, prev, cur)
                        if at and not L.proj and at[1] % 2 == 1:
                            n, h = at
                            dve.wait_ge(ptp_full.h, ptp_full.at(graph(i, n), h + 1))
                            v_.tensor_copy(L.pT[:, (H * (n % GP) + h) % NPT, :, :].rearrange("p k n -> p (k n)"),
                                           pt_ps[1][:]).then_inc(pt_dve.h, 1)

                def unit(i, u, prev, cur):
                    s, b = divmod(u % UNITS, GP)
                    g = stage_unit(i, u)
                    if cur:
                        for c in range(KC):
                            dve.wait_ge(proj_hi.h, proj_hi.at(g, c + 1))
                            low(L.xT[:, 1, c, :], proj_ps[(proj_full.per * u + c) % 2][:, 0:N], L.xT[:, 0, c, :]
                                ).then_inc(proj_free.h, 1)
                        for q in range(QT):
                            dve.wait_ge(sc_full.h, sc_full.at(g, q + 1))
                            v_.tensor_reduce(L.rowmax[:, q:q + 1], sc_ps[q][:, 0:N], AX.X, ALU.max
                                             ).then_inc(red_done.h, 1)
                            dve.wait_ge(red_done.h, red_done.at(g, q + 1))
                            v_.tensor_scalar(L.negmax[:, q:q + 1], L.rowmax[:, q:q + 1], -L.scale, None,
                                             ALU.mult).then_inc(max_ready.h, 1)
                        if s == 0:
                            dve.wait_ge(adj_loaded[b].h, adj_loaded[b].at(of_parity(i, b), 16))
                        for q in range(QT):
                            t = QT * b + q
                            dve.wait_ge(exp_done.h, exp_done.at(g, q + 1))
                            v_.tensor_tensor_reduce(L.delta[:, q, :], L.e[:, q, :], L.adj[:, t, :], 1.0, 0.0,
                                                    ALU.mult, ALU.add, L.dsum[:, q:q + 1]).then_inc(delta_ready.h, 1)
                            dve.wait_ge(delta_ready.h, delta_ready.at(g, q + 1))
                            v_.tensor_tensor_reduce(L.scr[:], L.delta[:, q, P * q:P * q + P], ident[:], 1.0, 0.0,
                                                    ALU.mult, ALU.add, L.diag[:, t:t + 1]).then_inc(d_step.h, 1)
                            v_.scalar_tensor_tensor(out=L.dsum[:, q:q + 1], in0=L.total[:, q:q + 1],
                                                    scalar=L2_SUM_EPS, in1=L.dsum[:, q:q + 1],
                                                    op0=ALU.mult, op1=ALU.add).then_inc(d_step.h, 1)
                            dve.wait_ge(d_step.h, d_step.at(g, 3 * q + 2))
                            v_.reciprocal(L.rdel[:, t:t + 1], L.dsum[:, q:q + 1]).then_inc(d_step.h, 1)
                    if prev:
                        ps_, pb = divmod((u - 1) % UNITS, GP)
                        gp = stage_unit(i, u - 1)
                        chain = Chain(gp)
                        dve.wait_ge(d_step.h, d_step.at(gp, 3 * QT))
                        for q in range(QT):
                            t = QT * pb + q
                            dve.wait_ge(att_full.h, att_full.at(gp, 2 + q))
                            v_.scalar_tensor_tensor(out=L.c[:, q, :], in0=L.hp[:, 1, t, :],
                                                    scalar=L.diag[:, t:t + 1],
                                                    in1=att_ps[(3 * (u - 1) + 1 + q) % 2][:, 0:D],
                                                    op0=ALU.mult, op1=ALU.add).then_inc(att_free.h, 1)
                        for q in range(QT):
                            t = QT * pb + q
                            dve.wait_ge(att_free.h, att_free.at(gp, 2 + q))
                            chain.step(v_.tensor_scalar(L.c[:, q, :], L.c[:, q, :], L.rdel[:, t:t + 1],
                                                        None, ALU.mult), wait=q == QT - 1)
                        chain.statistics([L.c[:, q, :] for q in range(QT)], L2_LN_EPS)
                        chain.newton()
                        for q in range(QT):
                            chain.step(v_.scalar_tensor_tensor(
                                out=L.c[:, q, :], in0=L.c[:, q, :], scalar=L.mv[:, q, 0:1],
                                in1=L.rows[:, ps_, 3, :], op0=ALU.subtract, op1=ALU.mult), wait=q == QT - 1)
                        for q in range(QT):
                            chain.step(v_.scalar_tensor_tensor(
                                out=L.c[:, q, :], in0=L.c[:, q, :], scalar=L.rstd[:, q:q + 1],
                                in1=L.rows[:, ps_, 4, :], op0=ALU.mult, op1=ALU.add), wait=q == QT - 1)
                        if ps_ == 0:
                            for q in range(QT):
                                last = q == QT - 1
                                chain.step(v_.tensor_scalar(L.h[:, QT * pb + q, :], L.c[:, q, :], 0.0, None,
                                                            ALU.max), wait=False,
                                           more=L.steps - L.sub_steps[0] if last else 0)
                            assert chain.n == L.steps, (chain.n, L.steps)
                        else:
                            n = -1 if u == 0 else 0
                            y_free(i, n)
                            dve.wait_ge(kept.h, kept.at(graph(i, n), 1))
                            for q in range(QT):
                                t = QT * pb + q
                                chain.step(v_.scalar_tensor_tensor(
                                    out=L.y[:, t, :], in0=L.c[:, q, :], scalar=0.0, in1=L.res[:, t, :],
                                    op0=ALU.max, op1=ALU.add), wait=q == QT - 1)
                            chain.layer_norm(pb)
                    if cur:
                        dve.wait_ge(att_full.h, att_full.at(g, 1))

                        def block_of(jt, it):
                            return att_ps[3 * u % 2][:, N * jt + P * it:N * jt + P * it + P]
                        v_.tensor_tensor(L.dT[:, 0, :], block_of(0, 0), behind[:], ALU.mult)
                        v_.tensor_tensor(L.dT[:, 2, :], block_of(1, 1), behind[:], ALU.mult)
                        v_.tensor_tensor(L.dT[:, 3, :], block_of(0, 0), before[:], ALU.mult)
                        v_.tensor_tensor(L.dT[:, 5, :], block_of(1, 1), before[:], ALU.mult)
                        v_.tensor_copy(L.dT[:, 1, :], block_of(1, 0))
                        v_.tensor_copy(L.dT[:, 4, :], block_of(0, 1)).then_inc(att_free.h, 1)

                if L.attn:
                    halves(dve, half)
                else:
                    units(dve, unit)
                leave(L)


def kernel(**inputs):
    import numpy as np
    import concourse.bacc as bacc
    from concourse.bass_utils import run_bass_kernel_spmd

    nc = bacc.Bacc("TRN2", target_bir_lowering=False, num_devices=1)
    arrays, aps = {}, {}

    def give(name, a):
        a = np.ascontiguousarray(a)
        arrays[name] = a
        aps[name] = nc.dram_tensor(name, a.shape, mybir.dt.from_np(a.dtype), kind="ExternalInput").ap()

    give("x", np.asarray(inputs["x"]).reshape(B * N, D))
    give("adj", inputs["adj"])
    for name, a in inputs.items():
        a = np.asarray(a)
        if name in ("x", "adj"):
            continue
        if name.startswith("L2_gnn_W"):
            for s in range(2):
                give(f"{name}{s}", a[s].T)
        elif name[:7] in ("L1_gnn_", "L3_gnn_") and name[7] == "W":
            give(name, a.T)
        elif name in ("L0_gnn_bk", "L0_gnn_bq"):
            give(name, a.reshape(J, KC, HD).transpose(0, 2, 1).reshape(P, KC))
        elif a.ndim == 0:
            give(name, a.reshape(1))
        else:
            give(name, a)
    out = nc.dram_tensor("out", (B * N, D), F32, kind="ExternalOutput").ap()
    build(nc, aps["x"], aps["adj"], aps, out)
    r = run_bass_kernel_spmd(nc, [arrays], core_ids=[0])
    return r.results[0]["out"].reshape(B, N, D)
```

```python
from contextlib import ExitStack

import concourse.bass as bass
from concourse import mybir

P = 128
B, N, D, H = 32, 256, 384, 12
HD = D // H
GP = 2
PAIRS = B // GP
QT = N // P
T = GP * QT
KC = D // P
J = P // HD
NH = GP * H
GROUPS = H // J
NPT = 8
NPB = 3
NSH = 3
STAGES = 4
SUBS = 2
UNITS = GP * SUBS
MASKED = 9.0e15
FMAX = 3.4e38
LN_EPS, L2_LN_EPS, L2_SUM_EPS = 1e-5, 1e-12, 1e-10
RSQRT_MAGIC = float(0x5F3759DF)
NEWTON = 3

ALU = mybir.AluOpType
ACT = mybir.ActivationFunctionType
F32 = mybir.dt.float32
F32R = mybir.dt.float32r
I32 = mybir.dt.int32
AX = mybir.AxisListType

ESTIMATE = 3
BEGUN = 2 * QT + ESTIMATE

LAG_T, LAG_PV = 2, 4
NAT, ONT = 4, 8
OUT, SUM, ESTIMATED, APPLY = 0, 1, 4, 7
KEEP_RES, KEEP_EDGE = 4, 2
FOLDS = 4
FOLDED = N // 4

PROJ_AT = {0: (0, 1), 1: (2,), 2: (3, 4), 3: (5,), 4: (6,), 5: (7,), 6: (8,), 8: (9,), 10: (10,)}
PROJ_USES = 3 * KC + QT
K_USE, Q_USE, V_USE = KC, 2 * KC, 3 * KC

HEADS_USE = {False: (3, 4, 5), True: (5, 8, 11)}
END_USE = {False: (6, 7), True: (12, 13, 15, 16, 18, 19)}
ATT_USES = {False: 5, True: 9}


class Sem:

    def __init__(self, handle, credit):
        self.h, self.credit, self.base, self.per = handle, credit, credit, 0

    def at(self, unit, k):
        i, per_iteration, n = unit
        return i * (per_iteration * self.per) + (self.base + n * self.per + k)


def graph(i, n):
    return (i, GP, n)


def of_parity(i, n):
    return (i, 1, n // GP)


def stage_unit(i, u):
    return (i, UNITS, u)


def wait_apart(eng, s, value):
    eng.wait_ge(s.h, value)
    eng.nop(nofuse=True)


class Norm:

    def __init__(self, sb, name):
        self.stats, self.mv = sb(name + "stats", [P, QT, 6]), sb(name + "mv", [P, QT, 2])
        self.var, self.half = sb(name + "var", [P, QT]), sb(name + "half", [P, QT], I32)
        self.rstd = sb(name + "rstd", [P, QT])


class Layer:

    def __init__(self, n):
        self.n = n
        self.attn = n != 2
        self.proj = n in (1, 3)
        if n == 0:
            self.mats = ["L0_gnn_Wk", "L0_gnn_Wq", "L0_gnn_Wv"]
            self.scale = HD ** -0.5
        elif n == 2:
            self.mats = [f"L2_gnn_{m}{s}" for s in range(SUBS) for m in ("Wl", "Ws", "Wr")]
            self.scale = D ** -0.5
        else:
            self.mats = [f"L{n}_gnn_{m}" for m in ("Wk", "Wq", "Wv", "Wo")]
            self.scale = D ** -0.5
        if self.proj:
            self.steps = 3 + BEGUN
        elif self.attn:
            self.steps = 1 + QT + BEGUN
        else:
            self.first_steps = QT + BEGUN
            self.sum_steps = self.first_steps + 3 * QT
            self.steps = self.sum_steps + BEGUN
        self.n_bias = {0: 4, 1: 2, 2: 10, 3: 2}[n]

    def alloc(self, sb, shared):
        n = f"L{self.n}_"
        self.x, self.res, self.adj, self.y = shared
        self.w_hi = sb(n + "w_hi", [P, len(self.mats), KC, D], F32R)
        self.w_lo = sb(n + "w_lo", [P, len(self.mats), KC, D], F32R)
        self.xT = sb(n + "xT", [P, 2, KC, N], F32R)
        self.unit_xT = (self.xT, None if self.attn else sb(n + "xT_odd", [P, 2, KC, N], F32R))
        self.norms = [Norm(sb, f"{n}{name}") for name in (("out_", "sub_") if n == "L2_" else ("out_",))]
        self.tmp = sb(n + "tmp", [P, QT])
        if self.attn:
            self.edge = sb(n + "edge", [P, T, N])
            self.negmax, self.total = sb(n + "negmax", [P, NH, QT]), sb(n + "total", [P, NH, QT])
            self.rz = sb(n + "rz", [P, NH, QT])
            self.probs = sb(n + "probs", [P, NPB, QT, N])
            self.kq_parts = sb(n + "kq_parts", [P, 4, KC, N], F32R)
            self.kq_stack = sb(n + "kq_stack", [3 * HD, GP, J, 2, KC, N], F32R)
            self.v = sb(n + "v", [P, T, D])
            self.v_bias = sb(n + "v_bias", [P, D])
            self.shifted = sb(n + "shifted", [P, NSH, QT, N])
            self.pT = sb(n + "pT", [P, NPT, QT, N])
            self.oT = sb(n + "oT", [P, GROUPS, N])
            self.o = sb(n + "o", [P, QT, D])
            if self.proj:
                self.absmax = sb(n + "absmax", [P, NH, QT])
                self.fold = sb(n + "fold", [P, QT, N // 2])
                self.folded = sb(n + "folded", [P, FOLDS, QT, FOLDED])
                self.onT = sb(n + "onT", [P, QT, 2, KC, P], F32R)
                self.o_bias = sb(n + "o_bias", [P, D])
            else:
                self.neg_beta = sb(n + "neg_beta", [P, 1])
                self.kq_bias = sb(n + "kq_bias", [P, 2, KC])
        else:
            self.h = sb(n + "h", [P, T, D])
            self.hp = sb(n + "hp", [P, 3, T, D])
            self.rows = sb(n + "rows", [P, SUBS, 5, D])
            self.e, self.delta = sb(n + "e", [P, QT, N]), sb(n + "delta", [P, QT, N])
            self.dT = sb(n + "dT", [P, 6, P])
            self.rowmax, self.negmax = sb(n + "rowmax", [P, QT]), sb(n + "negmax", [P, QT])
            self.total, self.dsum = sb(n + "total", [P, QT]), sb(n + "dsum", [P, QT])
            self.diag, self.rdel = sb(n + "diag", [P, T]), sb(n + "rdel", [P, T])
            self.scr = sb(n + "scr", [P, P])
            self.c = sb(n + "c", [P, QT, D])

    def bias_loads(self, w):
        n = f"L{self.n}_gnn_"

        def row(name):
            return w[name].rearrange("(a d) -> a d", a=1).broadcast_to([P, D])
        if self.n == 0:
            yield self.neg_beta[:], w[n + "beta"].rearrange("(a d) -> a d", a=1).broadcast_to([P, 1])
            yield self.v_bias[:], row(n + "bv")
            for kq, name in enumerate(("bk", "bq")):
                yield self.kq_bias[:, kq, :], w[n + name]
        elif self.n == 2:
            for s in range(SUBS):
                for m, name in enumerate(("bl", "bs", "br", "ln_w", "ln_b")):
                    yield self.rows[:, s, m, :], w[n + name][s:s + 1, :].broadcast_to([P, D])
        else:
            yield self.v_bias[:], row(n + "bv")
            yield self.o_bias[:], row(n + "bo")


PRODUCTS = ((0, 0), (0, 2), (1, 0), (1, 2), (0, 1), (1, 1))
EDGES_AT = 4
NEXT_AT = 4
BIASES_FIRST = 1


def halves(eng, half):
    half(-1, 1, False, False, True)
    half(0, 0, False, True, True)
    half(0, 1, True, True, True)
    with eng.Fori(1, PAIRS - 1) as i:
        half(i, 0, True, True, True)
        half(i, 1, True, True, True)
    half(PAIRS - 1, 0, True, True, True)
    half(PAIRS - 1, 1, True, True, False)
    half(PAIRS, 0, True, False, False)
    half(PAIRS, 1, False, False, False)


def units(eng, unit):
    def pair(i, before, last):
        order = [(0, 1), (1, 0), (0, 2), (1, 1)]
        hurried = 1 if isinstance(i, int) and i == 0 else None
        if isinstance(i, int) and i == PAIRS - 1:
            order.remove((0, 2))
            order += [None]
            hurried = 2
        following = [*order[1:], (0, GP + 1) if hurried != 2 else None]
        for u, (this, nxt) in enumerate(zip(order, following), 1):
            unit(i, u, this, nxt, before, last, u == hurried, u - 1 == hurried)
            before, last = this, before

    unit(0, 0, (0, 0), (0, 1), None, None, False, False)
    pair(0, (0, 0), None)
    with eng.Fori(1, PAIRS - 1) as i:
        pair(i, (1, -1), (0, 0))
    pair(PAIRS - 1, (1, -1), (0, 0))
    unit(PAIRS, 1, None, None, None, (1, -1), False, False)


def first_unit(i, n):
    if isinstance(i, int) and GP * i + n == 0:
        return (0, UNITS, 0)
    return (i, UNITS, SUBS * n - 1)


def is_graph(i, n):
    return not isinstance(i, int) or 0 <= GP * i + n < B


def head_at(i, b, s, lag, prev, cur):
    if s >= lag:
        return (b, s - lag) if cur else None
    return (b - 1, s - lag + H) if prev else None


def head_ahead(i, b, s, cur, nxt):
    if s < H - 1:
        return (b, s + 1) if cur else None
    return (b + 1, 0) if nxt else None


def build(nc, x_in, adj_in, w, out):
    ctx = ExitStack()
    with ctx:
        def sb(name, shape, dt=F32):
            return ctx.enter_context(nc.sbuf_tensor(name, shape, dt))

        sems = []

        def sem(name, credit=0):
            sems.append(Sem(ctx.enter_context(nc.semaphore(name)), credit))
            return sems[-1]

        def bank(name):
            return ctx.enter_context(nc.psum_tensor(name, [P, 512], F32))

        proj_ps = [bank(f"proj{r}") for r in range(2)]
        att_ps = [bank(f"att{r}") for r in range(2)]
        sc_ps = [bank(f"scores{r}") for r in range(2)]
        pt_ps = [bank(f"probsT{r}") for r in range(2)]

        ident = sb("ident", [P, P])
        ahead = sb("ahead", [P, P])
        behind = sb("behind", [P, P])

        init_done = sem("init_done")
        x_loaded = [sem(f"x_loaded{b}") for b in range(GP)]
        adj_loaded = [sem(f"adj_loaded{b}") for b in range(GP)]
        stored = [sem(f"stored{b}", 16) for b in range(GP)]
        w_loaded = [sem(f"w_loaded{m}") for m in range(STAGES)]
        b_loaded = sem("b_loaded")
        stacked = [sem(f"stacked{j}") for j in range(J)]
        w_hi, w_lo = sem("w_hi"), sem("w_lo")
        pool_step = sem("pool_step")
        edge_step = sem("edge_step")
        newton_step = sem("newton_step")
        kept = sem("kept")
        edge_ready = sem("edge_ready")
        rstd_ready = sem("rstd_ready")
        proj_full = sem("proj_full")
        x_full = sem("x_full")
        proj_hi = sem("proj_hi")
        proj_free = sem("proj_free", 2)
        proj_act = sem("proj_act", 2)
        heads_full = sem("heads_full")
        att_full = sem("att_full")
        oT_ready = sem("oT_ready")
        att_hi = sem("att_hi")
        att_free = sem("att_free", 2)
        sc_full = sem("sc_full")
        sc_read = sem("sc_read", 2)
        fold_half = sem("fold_half")
        fold_done = sem("fold_done", NSH)
        abs_done = sem("abs_done", 1)
        exp_done = sem("exp_done", NSH)
        ptp_full = sem("ptp_full", NPB)
        pt_act, pt_dve = sem("pt_act", 2), sem("pt_dve", 2)
        ln_step = sem("ln_step")
        y_ready = sem("y_ready", 2)
        red_done, max_ready = sem("red_done"), sem("max_ready")
        delta_ready = sem("delta_ready")
        d_step = sem("d_step")
        hp_ready = sem("hp_ready")

        xs = [x_in] + [nc.dram_tensor(f"x_after{n}", (B * N, D), F32, kind="Internal").ap()
                       for n in range(3)] + [out]
        adj_v = adj_in.rearrange("(n b) (q p) k -> b n p q k", b=GP, p=P)

        def nodes(ap):
            return ap.rearrange("(n b q p) d -> b n p q d", b=GP, q=QT, p=P)

        stage = sb("stage", [P, STAGES, KC, D])
        shared = [sb("x_tiles", [P, T, D]), sb("res", [P, T, D]), sb("adj_tiles", [P, T, N]), sb("y", [P, T, D])]
        layers = [Layer(n) for n in range(4)]
        all_mats = [name for L in layers for name in L.mats]
        for n, L in enumerate(layers):
            L.first = sum(len(before.mats) for before in layers[:n])
        for L in layers:
            with ExitStack() as own:
                L.alloc(lambda name, shape, dt=F32: own.enter_context(nc.sbuf_tensor(name, shape, dt)), shared)

        def enter(L):
            for b in range(GP):
                x_loaded[b].per = adj_loaded[b].per = stored[b].per = 16
            kept.per = y_ready.per = 1
            ln_step.per = L.steps
            if L.attn:
                for s in stacked:
                    s.per = 16 * 3
                proj_full.per, proj_hi.per = PROJ_USES, 3 * KC
                proj_free.per = PROJ_USES if L.proj else 3 * KC
                proj_act.per = 0 if L.proj else QT
                oT_ready.per = GROUPS
                att_free.per = (3 if L.proj else 1) * QT
                att_full.per = att_free.per
                heads_full.per = GROUPS
                att_hi.per = QT if L.proj else 0
                sc_full.per = sc_read.per = exp_done.per = ptp_full.per = H
                abs_done.per = H // 2 if L.proj else 0
                fold_half.per = fold_done.per = H if L.proj else 0
                edge_ready.per = rstd_ready.per = 1
                edge_step.per = 2 if L.n == 0 else 0
                newton_step.per = 4 * NEWTON
                pt_act.per, pt_dve.per = (H, 0) if L.proj else (H // 2, H // 2)
            else:
                x_full.per, proj_hi.per, proj_free.per = KC, KC, KC
                proj_full.per = proj_act.per = len(PRODUCTS)
                att_full.per = att_free.per = 1 + QT
                sc_full.per = exp_done.per = red_done.per = max_ready.per = delta_ready.per = QT
                d_step.per = 3 * QT
                hp_ready.per = 3 * QT
                newton_step.per = SUBS * 4 * NEWTON
                rstd_ready.per = SUBS

        def leave(L):
            for s in sems:
                s.base += s.per * PAIRS * (GP if L.attn else UNITS)
                s.per = 0
            for s in (*x_loaded, *adj_loaded, *stored):
                s.base -= 16 * PAIRS * ((GP if L.attn else UNITS) - 1)
            if not L.attn:
                for s in (kept, y_ready):
                    s.base -= PAIRS * (UNITS - GP)
            w_hi.base += len(L.mats)
            w_lo.base += len(L.mats)
            b_loaded.base += 16 * L.n_bias

        def heads_bank(L, n, gr):
            return att_ps[(ATT_USES[L.proj] * (n % GP) + HEADS_USE[L.proj][gr]) % 2]

        def end_bank(L, n, k):
            return att_ps[(ATT_USES[L.proj] * (n % GP) + END_USE[L.proj][k]) % 2]

        def unit_x(c):
            return pt_ps[c // 2][:, N * (c % 2):N * (c % 2) + N]

        def begin():
            for s in sems:
                s.base, s.per = s.credit, 0

        block = ctx.enter_context(nc.Block())

        @block.sync
        def _(sp):
            begin()
            for b in range(GP):
                sp.sem_inc(stored[b].h, 16)
            for L in layers:
                enter(L)
                src_x, dst_x = nodes(xs[L.n]), nodes(xs[L.n + 1])

                def load_x(i, n):
                    b = n % GP
                    sp.dma_start(L.x[:, QT * b:QT * b + QT, :], src_x[b][i + n // GP]).then_inc(x_loaded[b].h, 16)

                def load_adj(i, n):
                    b = n % GP
                    sp.dma_start(L.adj[:, QT * b:QT * b + QT, :], adj_v[b][i + n // GP]
                                 ).then_inc(adj_loaded[b].h, 16)

                def load(i, n):
                    load_x(i, n)
                    load_adj(i, n)

                def store(i, n):
                    b = n % GP
                    wait_apart(sp, y_ready, y_ready.at(graph(i, n), 1))
                    sp.dma_start(dst_x[b][i + n // GP], L.y[:, QT * b:QT * b + QT, :]).then_inc(stored[b].h, 16)

                def load_matrix(k):
                    if k >= STAGES:
                        sp.wait_ge(w_lo.h, k - STAGES + 1)
                    sp.dma_start(stage[:, k % STAGES, :, :],
                                 w[all_mats[k]].rearrange("(c p) n -> p c n", p=P)
                                 ).then_inc(w_loaded[k % STAGES].h, 16)

                def load_next(b):
                    sp.wait_ge(stored[b].h, stored[b].at(of_parity(PAIRS, b), 0))
                    sp.dma_start(L.x[:, 0:QT, :], dst_x[b][0]).then_inc(x_loaded[b].h, 16)
                    sp.dma_start(L.adj[:, 0:QT, :], adj_v[b][0]).then_inc(adj_loaded[b].h, 16)

                if L.n == 0:
                    load(0, 0)
                    for k in range(len(L.mats)):
                        load_matrix(k)
                else:
                    sp.wait_ge(y_ready.h, y_ready.base)
                for dst, src in L.bias_loads(w):
                    sp.dma_start(dst, src).then_inc(b_loaded.h, 16)
                for k in range(L.first + STAGES, L.first + len(L.mats)):
                    load_matrix(k)
                if L.n:
                    sp.wait_ge(stored[1].h, stored[1].base)
                load(0, 1)
                end = L.first + len(L.mats)
                for k in range(end, min(end + STAGES, len(all_mats))):
                    load_matrix(k)

                def half(i, b, prev, cur, nxt):
                    if is_graph(i, b) and is_graph(i, b + GP):
                        wait_apart(sp, kept, kept.at(graph(i, b), 1))
                        wait_apart(sp, edge_ready, edge_ready.at(graph(i, b), 1))
                        wait_apart(sp, proj_full, proj_full.at(graph(i, b), KC))
                        load(i, b + GP)
                    if nxt:
                        g, nb = graph(i, b + 1), (b + 1) % GP
                        wait_apart(sp, proj_free, proj_free.at(g, V_USE))
                        for j in range(J):
                            for r, (first, step) in enumerate(((0, 2), (0, 3), (1, 1))):
                                sp.dma_start(L.kq_stack[HD * r:HD * r + HD, nb, j, :, :, :].bitcast(F32),
                                             L.kq_parts[HD * j:HD * j + HD, first:first + step + 1:step, :, :]
                                             .bitcast(F32)).then_inc(stacked[j].h, 16)
                    if is_graph(i, b - 2):
                        store(i, b - 2)
                        if L.n < 3 and isinstance(i, int) and (i, b) == (PAIRS, 0):
                            load_next(0)

                def pair(i):
                    if is_graph(i, -1):
                        store(i, -1)
                    for n, second in ((3, False), (2, True), (4, False), (3, True)):
                        if second and n == 3:
                            store(i, 0)
                        if not is_graph(i, n):
                            continue
                        if second:
                            wait_apart(sp, delta_ready, delta_ready.at(stage_unit(i, 2 * (n - 1)), QT))
                            load_adj(i, n)
                        else:
                            wait_apart(sp, x_full, x_full.at(first_unit(i, n - GP), KC))
                            wait_apart(sp, kept, kept.at(graph(i, n - GP), 1))
                            load_x(i, n)

                if L.attn:
                    halves(sp, half)
                else:
                    sp.wait_ge(x_full.h, x_full.at(first_unit(0, 0), KC))
                    sp.wait_ge(kept.h, kept.at(graph(0, 0), 1))
                    load_x(0, GP)
                    pair(0)
                    with sp.Fori(1, PAIRS - 2) as i:
                        pair(i)
                    pair(PAIRS - 2)
                    pair(PAIRS - 1)
                    load_next(0)
                    store(PAIRS, -1)
                leave(L)
            for b in range(GP):
                sp.wait_ge(stored[b].h, stored[b].base)

        @block.gpsimd
        def _(pool):
            begin()
            g_ = nc.gpsimd
            pool.sem_inc(fold_done.h, NSH)
            g_.memset(ident[:], 0.0).then_inc(pool_step.h, 1)
            g_.memset(ahead[:], 1.0).then_inc(pool_step.h, 1)
            g_.memset(behind[:], 1.0).then_inc(pool_step.h, 1)
            pool.wait_ge(pool_step.h, 3)
            g_.affine_select(out=ident[:], in_=ident[:], compare_op=ALU.not_equal, fill=1.0, base=0,
                             pattern=[[-1, P]], channel_multiplier=1).then_inc(init_done.h, 1)
            g_.affine_select(out=ahead[:], in_=ahead[:], compare_op=ALU.is_gt, fill=0.0, base=0,
                             pattern=[[1, P]], channel_multiplier=-1).then_inc(init_done.h, 1)
            g_.affine_select(out=behind[:], in_=behind[:], compare_op=ALU.is_gt, fill=0.0, base=0,
                             pattern=[[-1, P]], channel_multiplier=1).then_inc(init_done.h, 1)
            def keep_residual(L, i, n, prev=False):
                g, b = graph(i, n), n % GP
                pool.wait_ge(x_loaded[b].h, x_loaded[b].at(of_parity(i, n), 16))
                if not L.attn:
                    if prev:
                        wait_apart(pool, ln_step, ln_step.at((i, UNITS, SUBS * n - 2), L.sum_steps))
                    pool.nop(nofuse=True)
                    tiles = slice(QT * b, QT * b + QT)
                    g_.tensor_copy(L.res[:, tiles, :], L.x[:, tiles, :]).then_inc(kept.h, 1)
                    return
                if prev:
                    if L.proj:
                        pool.wait_ge(att_free.h, att_free.at(graph(i, n - 2), 3 * QT))
                    else:
                        pool.wait_ge(ln_step.h, ln_step.at(graph(i, n - 2), L.steps - ESTIMATE - 2))
                row = L.o_bias if L.proj else L.v_bias
                for t in range(QT * b, QT * b + QT):
                    ins = g_.tensor_tensor(L.res[:, t, :], L.x[:, t, :], row[:], ALU.add)
                ins.then_inc(kept.h, 1)

            def keep_edge(L, i, n, prev):
                g, b = graph(i, n), n % GP
                tiles = slice(QT * b, QT * b + QT)
                if prev:
                    pool.wait_ge(sc_read.h, sc_read.at(g, -H))
                wait_apart(pool, adj_loaded[b], adj_loaded[b].at(of_parity(i, n), 16))
                if L.n == 0:
                    g_.tensor_scalar(L.edge[:, tiles, :], L.adj[:, tiles, :], 0.0, MASKED, ALU.is_le, ALU.mult
                                     ).then_inc(edge_step.h, 1)
                    g_.tensor_scalar(L.adj[:, tiles, :], L.adj[:, tiles, :], L.neg_beta[:], None, ALU.mult
                                     ).then_inc(edge_step.h, 1)
                    pool.wait_ge(edge_step.h, edge_step.at(g, 2))
                    g_.tensor_tensor(L.edge[:, tiles, :], L.edge[:, tiles, :], L.adj[:, tiles, :], ALU.add
                                     ).then_inc(edge_ready.h, 1)
                else:
                    g_.tensor_scalar(L.edge[:, tiles, :], L.adj[:, tiles, :], -1.0 if L.n == 1 else -2.0,
                                     None, ALU.mult).then_inc(edge_ready.h, 1)

            def newton(L, norm, g, estimated, first=0):
                pool.wait_ge(ln_step.h, ln_step.at(g, estimated))
                for step in range(first, first + 4 * NEWTON, 4):
                    g_.tensor_tensor(L.tmp[:], norm.rstd[:], norm.rstd[:], ALU.mult).then_inc(newton_step.h, 1)
                    pool.wait_ge(newton_step.h, newton_step.at(g, step + 1))
                    g_.tensor_tensor(L.tmp[:], L.tmp[:], norm.var[:], ALU.mult).then_inc(newton_step.h, 1)
                    wait_apart(pool, newton_step, newton_step.at(g, step + 2))
                    g_.tensor_scalar(L.tmp[:], L.tmp[:], -0.5, 1.5, ALU.mult, ALU.add).then_inc(newton_step.h, 1)
                    pool.wait_ge(newton_step.h, newton_step.at(g, step + 3))
                    g_.tensor_tensor(norm.rstd[:], norm.rstd[:], L.tmp[:], ALU.mult).then_inc(newton_step.h, 1)
                    pool.wait_ge(newton_step.h, newton_step.at(g, step + 4))
                pool.sem_inc(rstd_ready.h, 1)

            def half(L, i, b, prev, cur, nxt):
                for s in range(H):
                    at = head_ahead(i, b, s, cur, nxt)
                    if at and L.proj:
                        g, h = graph(i, at[0]), at[1]
                        pool.wait_ge(fold_done.h, fold_done.at(g, h))
                        pool.wait_ge(sc_read.h, sc_read.at(g, h + 1))
                        g_.tensor_tensor(L.fold[:], L.shifted[:, h % NSH, :, 0:N // 2],
                                         L.shifted[:, h % NSH, :, N // 2:N], ALU.add).then_inc(fold_half.h, 1)
                        pool.wait_ge(abs_done.h, abs_done.at(g, h // 2 + 1 - FOLDS // 2))
                        pool.wait_ge(fold_half.h, fold_half.at(g, h + 1))
                        g_.tensor_tensor(L.folded[:, h % FOLDS, :, :], L.fold[:, :, 0:FOLDED],
                                         L.fold[:, :, FOLDED:2 * FOLDED], ALU.add).then_inc(fold_done.h, 1)
                    if nxt and s == KEEP_EDGE:
                        keep_edge(L, i, b + 1, prev)
                    if cur and s == KEEP_RES:
                        keep_residual(L, i, b, is_graph(i, b - 2))
                    if is_graph(i, b - 2) and s == ESTIMATED:
                        newton(L, L.norms[0], graph(i, b - 2), L.steps)

            for L in layers:
                enter(L)
                pool.wait_ge(b_loaded.h, b_loaded.base + 16 * L.n_bias)
                if L.n == 0:
                    g_.tensor_scalar(L.neg_beta[:], L.neg_beta[:], -1.0, None, ALU.mult).then_inc(pool_step.h, 1)
                    pool.wait_ge(pool_step.h, 4)
                if L.attn:
                    halves(pool, lambda *a: half(L, *a))
                else:
                    def unit(i, u, this, nxt, before, last, early, done):
                        def biases(ns):
                            for n in ns:
                                q, m = PRODUCTS[n]
                                pool.wait_ge(proj_act.h, proj_act.at(stage_unit(i, u), n + 1))
                                hp = L.hp[:, m, QT * (u % 2) + q, :]
                                g_.tensor_tensor(hp, hp, L.rows[:, this[0], m, :], ALU.add
                                                 ).then_inc(hp_ready.h, 1)
                        gp = stage_unit(i, u - 1)
                        if last and last[0] == 1:
                            newton(L, L.norms[0], stage_unit(i, u - 2), L.steps, 4 * NEWTON)
                        if this:
                            biases(range(BIASES_FIRST))
                        if before:
                            newton(L, L.norms[1], gp, L.first_steps)
                            if before[0] == 0:
                                pool.sem_inc(rstd_ready.h, 1)
                                pool.sem_inc(newton_step.h, 4 * NEWTON)
                        if this:
                            biases(range(BIASES_FIRST, len(PRODUCTS)))
                            if this[0] == 0:
                                keep_residual(L, i, this[1], is_graph(i, this[1] - GP))
                    units(pool, unit)
                leave(L)

        @block.tensor
        def _(pe):
            begin()
            pe.sem_inc(ptp_full.h, NPB)
            pe.wait_ge(init_done.h, 3)
            t_ = nc.tensor

            def parts3(ps, lhsT, rhs):
                terms = [(c, a, b) for c in range(KC) for a, b in ((0, 0), (0, 1), (1, 0))]
                for n, (c, a, b) in enumerate(terms):
                    mm = t_.matmul(ps, lhsT(a, c), rhs(b, c), start=n == 0, stop=n == len(terms) - 1)
                return mm

            for L in layers:
                enter(L)
                if L.n:
                    pe.wait_ge(y_ready.h, y_ready.base)

                def w_part(m):
                    return lambda a, c: (L.w_hi, L.w_lo)[a][:, m, c, :]

                def transpose_chunk(ps, src, b, c):
                    for q in range(QT):
                        mm = t_.transpose(ps[:, P * q:P * q + P], src[:, QT * b + q, P * c:P * c + P], ident[:])
                    return mm

                def project(i, n, u):
                    g, b = graph(i, n), n % GP
                    ps = proj_ps[(PROJ_USES * b + u) % 2]
                    free = proj_free if L.proj or u >= 2 else proj_act
                    pe.wait_ge(free.h, free.at(g, u - 1))
                    if u == 0:
                        pe.wait_ge(x_loaded[b].h, x_loaded[b].at(of_parity(i, n), 16))
                    if isinstance(i, int) and i < 0 and u in (K_USE, Q_USE, V_USE):
                        pe.wait_ge(w_lo.h, w_lo.base + (len(L.mats) if u == V_USE else u // KC))
                    if u < K_USE:
                        mm = transpose_chunk(ps, L.x, b, u)
                    elif u < V_USE:
                        if u == K_USE:
                            pe.wait_ge(proj_free.h, proj_free.at(g, KC))
                        m, c = divmod(u - K_USE, KC)
                        mm = parts3(ps[:, 0:N], lambda a, k: w_part(m)(a, k)[:, P * c:P * c + P],
                                    lambda a, k: L.xT[:, a, k, :])
                    else:
                        q = u - V_USE
                        mm = parts3(ps[:, 0:D], lambda a, k: L.xT[:, a, k, P * q:P * q + P], w_part(2))
                    mm.then_inc(proj_full.h, 1)

                def scores(g, b, h):
                    j, c = divmod(h, KC)
                    if c == 0:
                        pe.wait_ge(stacked[j].h, stacked[j].at(g, 16 * 3))
                    pe.wait_ge(sc_read.h, sc_read.at(g, h + 1 - 2))
                    for q in range(QT):
                        mm = t_.matmul(sc_ps[h % 2][:, N * q:N * q + N],
                                       L.kq_stack[:, b, j, 1, c, P * q:P * q + P],
                                       L.kq_stack[:, b, j, 0, c, :], start=True, stop=True)
                    mm.then_inc(sc_full.h, 1)

                def half(i, b, prev, cur, nxt):
                    for s in range(H):
                        at = head_ahead(i, b, s, cur, nxt)
                        if at:
                            scores(graph(i, at[0]), at[0] % GP, at[1])
                        at = head_at(i, b, s, LAG_T, prev, cur)
                        if at:
                            n, h = at
                            g = graph(i, n)
                            pe.wait_ge(exp_done.h, exp_done.at(g, h + 1))
                            if L.proj:
                                pe.wait_ge(pt_act.h, pt_act.at(g, h - 1))
                            else:
                                ev = (pt_act, pt_dve)[h % 2]
                                pe.wait_ge(ev.h, ev.at(g, h // 2))
                            for kt in range(QT):
                                for q in range(QT):
                                    mm = t_.transpose(pt_ps[h % 2][:, N * kt + P * q:N * kt + P * q + P],
                                                      L.probs[:, h % NPB, q, P * kt:P * kt + P], ident[:])
                            mm.then_inc(ptp_full.h, 1)
                        at = head_at(i, b, s, LAG_PV, prev, cur)
                        if at and at[1] % J == J - 1:
                            n, h = at
                            g, nb, gr = graph(i, n), n % GP, h // J
                            if L.proj:
                                pe.wait_ge(pt_act.h, pt_act.at(g, h + 1))
                            else:
                                pe.wait_ge(pt_act.h, pt_act.at(g, h // 2 + 1))
                                pe.wait_ge(pt_dve.h, pt_dve.at(g, h // 2 + 1))
                            if gr == 0:
                                if L.proj:
                                    pe.wait_ge(proj_free.h, proj_free.at(g, PROJ_USES))
                                else:
                                    pe.wait_ge(proj_act.h, proj_act.at(g, QT))
                            if gr == GROUPS - 1 and not L.proj:
                                pe.wait_ge(oT_ready.h, oT_ready.at(g, 1))
                            elif gr == GROUPS - 1:
                                if is_graph(i, n - 1):
                                    pe.wait_ge(att_free.h, att_free.at(graph(i, n - 1), 2 * QT + 1))
                            elif is_graph(i, n - 1):
                                pe.wait_ge(att_free.h, att_free.at(graph(i, n - 1), 1 + gr * (QT if L.proj else 1)))
                            ps = heads_bank(L, n, gr)
                            for kt in range(QT):
                                for k in range(J):
                                    hh = J * gr + k
                                    mm = t_.matmul(ps[HD * k:HD * k + HD, 0:N],
                                                   L.v[:, QT * nb + kt, HD * hh:HD * hh + HD],
                                                   L.pT[:, (H * nb + hh) % NPT, kt, :],
                                                   start=kt == 0, stop=kt == QT - 1)
                            mm.then_inc(heads_full.h, 1)
                        if prev and s == NAT:
                            pe.wait_ge(oT_ready.h, oT_ready.at(graph(i, b - 1), GROUPS))
                            if L.proj and is_graph(i, b - 2):
                                pe.wait_ge(att_free.h, att_free.at(graph(i, b - 2), 3 * QT))
                            for q in range(QT):
                                ps = end_bank(L, b - 1, q)
                                for gr in range(GROUPS):
                                    mm = t_.transpose(ps[:, P * gr:P * gr + P], L.oT[:, gr, P * q:P * q + P], ident[:])
                                mm.then_inc(att_full.h, 1)
                        if prev and L.proj and s == ONT:
                            pe.wait_ge(att_free.h, att_free.at(graph(i, b - 1), QT))
                            for q in range(QT):
                                ps = end_bank(L, b - 1, QT + q)
                                if cur and q == 1:
                                    pe.wait_ge(oT_ready.h, oT_ready.at(graph(i, b), 1))
                                for c in range(KC):
                                    mm = t_.transpose(ps[:, P * c:P * c + P], L.o[:, q, P * c:P * c + P], ident[:])
                                mm.then_inc(att_full.h, 1)
                        if is_graph(i, b - 2) and L.proj and OUT <= s < OUT + QT:
                            q = s - OUT
                            pe.wait_ge(att_free.h, att_free.at(graph(i, b - 2), 2 * QT))
                            if prev and q == 1:
                                pe.wait_ge(oT_ready.h, oT_ready.at(graph(i, b - 1), 2))
                            parts3(end_bank(L, b - 2, 2 * QT + q)[:, 0:D], lambda a, k: L.onT[:, q, a, k, :],
                                   w_part(3)).then_inc(att_full.h, 1)
                        if nxt:
                            for u in PROJ_AT.get(s, ()):
                                project(i, b + 1, u)

                def unit(i, u, this, nxt, before, last, early, done):
                    g, gp = stage_unit(i, u), stage_unit(i, u - 1)
                    xT = L.unit_xT[u % 2]

                    def begin_unit(u, what):
                        s, n = what
                        b, g = n % GP, stage_unit(i, u)
                        if s == 0:
                            pe.wait_ge(x_loaded[b].h, x_loaded[b].at(of_parity(i, n), 16))
                        else:
                            pe.wait_ge(ln_step.h, ln_step.at(first_unit(i, n), L.steps))
                        pe.wait_ge(proj_free.h, proj_free.at(g, 0))
                        for c in range(KC):
                            for q in range(QT):
                                mm = t_.transpose(unit_x(c)[:, P * q:P * q + P],
                                                  (L.h if s else L.x)[:, QT * b + q, P * c:P * c + P], ident[:])
                            mm.then_inc(x_full.h, 1)

                    if this and (done or u == 0):
                        begin_unit(u, this)
                    if this:
                        s, n = this
                        pe.wait_ge(proj_free.h, proj_free.at(g, KC))
                        for q in range(QT):
                            pe.wait_ge(exp_done.h, exp_done.at(g, q + 1 - 2))
                            parts3(sc_ps[q][:, 0:N], lambda a, k: xT[:, a, k, P * q:P * q + P],
                                   lambda a, k: xT[:, a, k, :]).then_inc(sc_full.h, 1)
                    if before:
                        pe.wait_ge(att_free.h, att_free.at(gp, 1))
                        pe.wait_ge(hp_ready.h, hp_ready.at(gp, 2 * QT))
                        for it in range(QT):
                            ps = att_ps[(3 * (u - 1) + 1 + it) % 2]
                            for n_, (blk, m, jt) in enumerate([((0, 0, 0), (1, 0, 1), (3, 2, 0)),
                                                               ((2, 0, 1), (4, 2, 0), (5, 2, 1))][it]):
                                mm = t_.matmul(ps[:, 0:D], L.dT[:, blk, :], L.hp[:, m, QT * ((u - 1) % 2) + jt, :],
                                               start=n_ == 0, stop=n_ == 2)
                            mm.then_inc(att_full.h, 1)
                    if this:
                        for k, (q, m) in enumerate(PRODUCTS):
                            if k == EDGES_AT:
                                pe.wait_ge(delta_ready.h, delta_ready.at(g, QT))
                                pe.wait_ge(att_free.h, att_free.at(g, -1))
                                for jt in range(QT):
                                    for it in range(QT):
                                        mm = t_.transpose(att_ps[3 * u % 2][:, N * jt + P * it:N * jt + P * it + P],
                                                          L.delta[:, it, P * jt:P * jt + P], ident[:])
                                mm.then_inc(att_full.h, 1)
                            if k == NEXT_AT and nxt and not early:
                                begin_unit(u + 1, nxt)
                            pe.wait_ge(proj_act.h, proj_act.at(g, k - 1))
                            parts3(proj_ps[k % 2][:, 0:D], lambda a, c: xT[:, a, c, P * q:P * q + P],
                                   w_part(3 * s + m)).then_inc(proj_full.h, 1)

                if not L.attn:
                    pe.wait_ge(w_lo.h, w_lo.base + len(L.mats))
                if L.attn:
                    halves(pe, half)
                else:
                    units(pe, unit)
                leave(L)

        @block.scalar
        def _(act):
            begin()
            act.sem_inc(exp_done.h, NSH)
            act.sem_inc(pt_act.h, 2)
            act.sem_inc(proj_act.h, 2)
            a_ = nc.scalar
            for L in layers:
                enter(L)
                for m in range(len(L.mats)):
                    number = L.first + m
                    act.wait_ge(w_loaded[number % STAGES].h, 16 * (number // STAGES + 1))
                    if L.n and m == 0:
                        act.wait_ge(y_ready.h, y_ready.base)
                    kq = L.attn and m < 2
                    f = -L.scale if L.attn and m == 1 else 1.0
                    for c in range(KC):
                        src, dst = stage[:, number % STAGES, c, :], L.w_hi[:, m, c, :]
                        if kq:
                            for k in range(KC):
                                ins = a_.activation(dst[:, P * k:P * k + P].rearrange("p (j d) -> p j d", j=J),
                                                    src.rearrange("p (j c d) -> p c j d", j=J, c=KC)[:, k],
                                                    ACT.Copy, scale=f)
                        else:
                            ins = a_.activation(dst, src, ACT.Copy, scale=f)
                    ins.then_inc(w_hi.h, 1)
                if L.n == 0:
                    act.wait_ge(b_loaded.h, b_loaded.base + 16 * L.n_bias)
                    act.wait_ge(w_lo.h, w_lo.base + len(L.mats))

                def project(i, n, u):
                    g, b = graph(i, n), n % GP
                    ps = proj_ps[(PROJ_USES * b + u) % 2]
                    if u >= V_USE and L.proj:
                        return
                    act.wait_ge(proj_full.h, proj_full.at(g, u + 1))
                    if u >= V_USE:
                        a_.activation(L.v[:, QT * b + u - V_USE, :], ps[:, 0:D], ACT.Copy).then_inc(proj_act.h, 1)
                    elif u < K_USE:
                        a_.activation(L.xT[:, 0, u, :], ps[:, 0:N], ACT.Copy).then_inc(proj_hi.h, 1)
                    else:
                        m, c = divmod(u - K_USE, KC)
                        if u == K_USE:
                            for j in range(J):
                                act.wait_ge(stacked[j].h, stacked[j].at(g, 0))
                        if L.n == 0:
                            a_.activation(L.kq_parts[:, 2 * m, c, :], ps[:, 0:N], ACT.Identity,
                                          bias=L.kq_bias[:, m, c:c + 1]).then_inc(proj_hi.h, 1)
                        else:
                            a_.activation(L.kq_parts[:, 2 * m, c, :], ps[:, 0:N], ACT.Copy).then_inc(proj_hi.h, 1)

                def half(i, b, prev, cur, nxt):
                    for s in range(H):
                        if nxt:
                            for u in PROJ_AT.get(s - 1, ()):
                                project(i, b + 1, u)
                        if cur:
                            g = graph(i, b)
                            act.wait_ge(sc_read.h, sc_read.at(g, s + 1))
                            act.wait_ge(ptp_full.h, ptp_full.at(g, s + 1 - NPB))
                            for q in range(QT):
                                ins = a_.activation(L.probs[:, s % NPB, q, :], L.shifted[:, s % NSH, q, :],
                                                    ACT.Exp, scale=-1.0, bias=L.negmax[:, H * b + s, q:q + 1],
                                                    accum_out=L.total[:, H * b + s, q:q + 1])
                            ins.then_inc(exp_done.h, 1)
                        if prev and L.proj and s == ONT + 1:
                            for q in range(QT):
                                u = QT + q
                                act.wait_ge(att_full.h, att_full.at(graph(i, b - 1), u + 1))
                                a_.activation(L.onT[:, q, 0, :, :].rearrange("p c n -> p (c n)"),
                                              end_bank(L, b - 1, u)[:, 0:D], ACT.Copy
                                              ).then_inc(att_hi.h, 1)
                        at = head_at(i, b, s, LAG_T, prev, cur)
                        if at and (L.proj or at[1] % 2 == 0):
                            n, h = at
                            act.wait_ge(ptp_full.h, ptp_full.at(graph(i, n), h + 1))
                            a_.activation(L.pT[:, (H * (n % GP) + h) % NPT, :, :].rearrange("p k n -> p (k n)"),
                                          pt_ps[h % 2][:], ACT.Copy).then_inc(pt_act.h, 1)
                        at = head_at(i, b, s, LAG_PV, prev, cur)
                        if at and at[1] % J == J - 1:
                            n, gr = at[0], at[1] // J
                            act.wait_ge(heads_full.h, heads_full.at(graph(i, n), gr + 1))
                            a_.activation(L.oT[:, gr, :], heads_bank(L, n, gr)[:, 0:N],
                                          ACT.Copy).then_inc(oT_ready.h, 1)

                def unit(i, u, this, nxt, before, last, early, done):
                    if not this:
                        return
                    g = stage_unit(i, u)

                    def begin_unit(u):
                        for c in range(KC):
                            act.wait_ge(x_full.h, x_full.at(stage_unit(i, u), max(c + 1, 2)))
                            a_.activation(L.unit_xT[u % 2][:, 0, c, :], unit_x(c), ACT.Copy
                                          ).then_inc(proj_hi.h, 1)

                    if done or u == 0:
                        begin_unit(u)
                    for q in range(QT):
                        act.wait_ge(max_ready.h, max_ready.at(g, q + 1))
                        a_.activation(L.e[:, q, :], sc_ps[q][:, 0:N], ACT.Exp, scale=L.scale,
                                      bias=L.negmax[:, q:q + 1], accum_out=L.total[:, q:q + 1]
                                      ).then_inc(exp_done.h, 1)
                    if not (isinstance(i, int) and i == 0 and u < 2):
                        act.wait_ge(att_free.h, att_free.at(stage_unit(i, u - 2), 1 + QT))
                    for k, (q, m) in enumerate(PRODUCTS):
                        if k == NEXT_AT and nxt and not early:
                            begin_unit(u + 1)
                        act.wait_ge(proj_full.h, proj_full.at(g, k + 1))
                        a_.activation(L.hp[:, m, QT * (u % 2) + q, :], proj_ps[k % 2][:, 0:D],
                                      ACT.Copy).then_inc(proj_act.h, 1)

                if L.attn:
                    halves(act, half)
                else:
                    units(act, unit)
                leave(L)

        @block.vector
        def _(dve):
            begin()
            dve.sem_inc(proj_free.h, 2)
            dve.sem_inc(att_free.h, 2)
            dve.sem_inc(sc_read.h, 2)
            dve.sem_inc(pt_dve.h, 2)
            dve.sem_inc(y_ready.h, 2)
            dve.sem_inc(abs_done.h, 1)
            v_ = nc.vector
            dve.wait_ge(init_done.h, 3)
            for L in layers:
                enter(L)
                for m in range(len(L.mats)):
                    dve.wait_ge(w_hi.h, w_hi.base + m + 1)
                    kq = L.attn and m < 2
                    f = -L.scale if L.attn and m == 1 else 1.0
                    if L.n == 0 and m == 1:
                        dve.wait_ge(b_loaded.h, b_loaded.base + 16 * L.n_bias)
                        v_.tensor_scalar(L.kq_bias[:, 1, :], L.kq_bias[:, 1, :], f, None, ALU.mult)
                    for c in range(KC):
                        src, hi, dst = stage[:, (L.first + m) % STAGES, c, :], L.w_hi[:, m, c, :], L.w_lo[:, m, c, :]
                        if kq:
                            for k in range(KC):
                                sl = slice(P * k, P * k + P)
                                ins = v_.scalar_tensor_tensor(
                                    out=dst[:, sl].rearrange("p (j d) -> p j d", j=J),
                                    in0=src.rearrange("p (j c d) -> p c j d", j=J, c=KC)[:, k], scalar=f,
                                    in1=hi[:, sl].bitcast(F32).rearrange("p (j d) -> p j d", j=J),
                                    op0=ALU.mult, op1=ALU.subtract)
                        else:
                            ins = v_.scalar_tensor_tensor(out=dst, in0=src, scalar=f, in1=hi.bitcast(F32),
                                                          op0=ALU.mult, op1=ALU.subtract)
                    ins.then_inc(w_lo.h, 1)
                dve.wait_ge(b_loaded.h, b_loaded.base + 16 * L.n_bias)
                dve.wait_ge(w_lo.h, w_lo.base + len(L.mats))

                class Chain:

                    def __init__(self, unit, n=0, norm=0):
                        self.unit, self.n, self.norm = unit, n, L.norms[norm]

                    def step(self, ins, wait=True, more=0):
                        self.n += 1 + more
                        ins.then_inc(ln_step.h, 1 + more)
                        if wait:
                            self.wait()

                    def wait(self, but=0):
                        wait_apart(dve, ln_step, ln_step.at(self.unit, self.n - but))

                    def estimate(self, eps):
                        self.wait()
                        self.step(v_.tensor_scalar(self.norm.var[:], self.norm.mv[:, :, 1], eps, None, ALU.add))
                        self.step(v_.tensor_scalar(self.norm.half[:], self.norm.var[:].bitcast(I32), 1, None,
                                                   ALU.logical_shift_right))
                        self.step(v_.tensor_scalar(self.norm.rstd[:].bitcast(I32), self.norm.half[:], -1.0, RSQRT_MAGIC,
                                                   ALU.mult, ALU.add), wait=False)

                    def statistics(self, tiles, eps):
                        for q, tile in enumerate(tiles):
                            self.wait(1)
                            self.step(v_.bn_stats(self.norm.stats[:, q, :], tile), wait=False)
                        for q in range(QT):
                            self.wait(1)
                            self.step(v_.bn_aggr(self.norm.mv[:, q, :], self.norm.stats[:, q, :]), wait=False)
                        self.estimate(eps)

                    def statistics_of(self, q, tile):
                        self.wait()
                        self.step(v_.bn_stats(self.norm.stats[:, q, :], tile))
                        self.step(v_.bn_aggr(self.norm.mv[:, q, :], self.norm.stats[:, q, :]), wait=False)

                def apply(b):
                    for q in range(QT):
                        tile = L.y[:, QT * b + q, :]
                        ins = v_.tensor_scalar(tile, tile, L.norms[0].mv[:, q, 0:1], L.norms[0].rstd[:, q:q + 1],
                                               ALU.subtract, ALU.mult)
                    ins.then_inc(y_ready.h, 1)

                def y_free(i, n):
                    dve.wait_ge(stored[n % GP].h, stored[n % GP].at(of_parity(i, n), 0))

                def low(dst, ps, hi, bias=None):
                    hi = hi.bitcast(F32)
                    if bias is None:
                        return v_.tensor_tensor(dst, ps, hi, ALU.subtract)
                    return v_.scalar_tensor_tensor(out=dst, in0=ps, scalar=bias, in1=hi,
                                                   op0=ALU.add, op1=ALU.subtract)

                def project(i, n, u):
                    g, b = graph(i, n), n % GP
                    ps = proj_ps[(PROJ_USES * b + u) % 2]
                    if u >= V_USE:
                        if L.proj:
                            dve.wait_ge(proj_full.h, proj_full.at(g, u + 1))
                            v_.tensor_tensor(L.v[:, QT * b + u - V_USE, :], ps[:, 0:D], L.v_bias[:], ALU.add
                                             ).then_inc(proj_free.h, 1)
                        return
                    dve.wait_ge(proj_hi.h, proj_hi.at(g, u + 1))
                    if u < K_USE:
                        ins = low(L.xT[:, 1, u, :], ps[:, 0:N], L.xT[:, 0, u, :])
                    else:
                        m, c = divmod(u - K_USE, KC)
                        ins = low(L.kq_parts[:, 2 * m + 1, c, :], ps[:, 0:N], L.kq_parts[:, 2 * m, c, :],
                                  L.kq_bias[:, m, c:c + 1] if L.n == 0 else None)
                    ins.then_inc(proj_free.h, 1)

                def half(i, b, prev, cur, nxt):
                    gp, pb = graph(i, b - 1), (b - 1) % GP
                    gpp, ppb = graph(i, b - 2), b % GP
                    if prev:
                        chain = Chain(gp)
                    if is_graph(i, b - 2):
                        ending = Chain(gpp, 3 if L.proj else 1)
                    for s in range(H):
                        at = head_ahead(i, b, s, cur, nxt)
                        if at:
                            n, h = at
                            g = graph(i, n)
                            if h == 0:
                                dve.wait_ge(edge_ready.h, edge_ready.at(g, 1))
                            dve.wait_ge(sc_full.h, sc_full.at(g, h + 1))
                            wait_apart(dve, exp_done, exp_done.at(g, h + 1 - NSH))
                            if L.proj:
                                wait_apart(dve, fold_done, fold_done.at(g, h + 1 - NSH))
                            for q in range(QT):
                                ins = v_.tensor_tensor_reduce(
                                    L.shifted[:, h % NSH, q, :], sc_ps[h % 2][:, N * q:N * q + N],
                                    L.edge[:, QT * (n % GP) + q, :], 1.0, FMAX, ALU.add, ALU.min,
                                    L.negmax[:, H * (n % GP) + h, q:q + 1])
                            ins.then_inc(sc_read.h, 1)
                        if nxt:
                            for u in PROJ_AT.get(s - 1, ()):
                                project(i, b + 1, u)
                        at = head_at(i, b, s, 2, prev, cur)
                        if at and L.proj and at[1] % 2 == 1:
                            n, h = at
                            hb = H * (n % GP) + h
                            wait_apart(dve, fold_done, fold_done.at(graph(i, n), h + 1))
                            v_.tensor_reduce(L.absmax[:, hb - 1:hb + 1, :],
                                             L.folded[:, h % FOLDS - 1:h % FOLDS + 1, :, :], AX.X, ALU.max
                                             ).then_inc(abs_done.h, 1)
                        if is_graph(i, b - 2) and SUM < s <= SUM + QT:
                            q = s - 1 - SUM
                            if L.proj:
                                dve.wait_ge(att_free.h, att_free.at(gpp, 2 * QT + q + 1))
                            ending.statistics_of(q, L.y[:, QT * ppb + q, :])
                        if is_graph(i, b - 2) and SUM <= s < SUM + QT:
                            q = s - SUM
                            t = QT * ppb + q
                            if q == 0:
                                y_free(i, b - 2)
                                dve.wait_ge(kept.h, kept.at(gpp, 1))
                            if L.proj:
                                dve.wait_ge(att_full.h, att_full.at(gpp, 2 * QT + q + 1))
                                v_.tensor_tensor(L.y[:, t, :], end_bank(L, b - 2, 2 * QT + q)[:, 0:D],
                                                 L.res[:, t, :], ALU.add).then_inc(att_free.h, 1)
                            else:
                                dve.wait_ge(att_free.h, att_free.at(gpp, q + 1))
                                ending.step(v_.tensor_tensor(L.y[:, t, :], L.o[:, q, :], L.res[:, t, :], ALU.add),
                                            wait=False)
                        if is_graph(i, b - 2) and s == ESTIMATED:
                            ending.estimate(LN_EPS)
                            assert ending.n == L.steps
                        if is_graph(i, b - 2) and s == APPLY:
                            wait_apart(dve, rstd_ready, rstd_ready.at(gpp, 1))
                            apply(ppb)
                        if prev and s == NAT:
                            hs = slice(H * pb, H * pb + H)
                            dve.wait_ge(exp_done.h, exp_done.at(gp, H))
                            chain.step(v_.reciprocal(L.rz[:, hs, :], L.total[:, hs, :]), wait=False)
                            if L.proj:
                                dve.wait_ge(abs_done.h, abs_done.at(gp, H // 2))
                                chain.step(v_.scalar_tensor_tensor(
                                    out=L.absmax[:, hs, :], in0=L.negmax[:, hs, :], scalar=0.0,
                                    in1=L.absmax[:, hs, :], op0=ALU.not_equal, op1=ALU.max))
                                chain.step(v_.scalar_tensor_tensor(
                                    out=L.rz[:, hs, :], in0=L.absmax[:, hs, :], scalar=0.0,
                                    in1=L.rz[:, hs, :], op0=ALU.is_gt, op1=ALU.mult), wait=False)
                        if prev and s == NAT + 1:
                            chain.wait()
                            hs = slice(H * pb, H * pb + H)
                            for q in range(QT):
                                dve.wait_ge(att_full.h, att_full.at(gp, q + 1))
                                v_.tensor_tensor(
                                    L.o[:, q, :].rearrange("p (h d) -> p h d", h=H),
                                    end_bank(L, b - 1, q)[:, 0:D].rearrange("p (h d) -> p h d", h=H),
                                    L.rz[:, hs, q:q + 1].broadcast_to([P, H, HD]), ALU.mult
                                ).then_inc(att_free.h, 1)
                        if prev and L.proj and s == ONT + 1:
                            for q in range(QT):
                                dve.wait_ge(att_hi.h, att_hi.at(gp, q + 1))
                                low(L.onT[:, q, 1, :, :].rearrange("p c n -> p (c n)"),
                                    end_bank(L, b - 1, QT + q)[:, 0:D],
                                    L.onT[:, q, 0, :, :].rearrange("p c n -> p (c n)")).then_inc(att_free.h, 1)
                        at = head_at(i, b, s, LAG_T, prev, cur)
                        if at and not L.proj and at[1] % 2 == 1:
                            n, h = at
                            dve.wait_ge(ptp_full.h, ptp_full.at(graph(i, n), h + 1))
                            v_.tensor_copy(L.pT[:, (H * (n % GP) + h) % NPT, :, :].rearrange("p k n -> p (k n)"),
                                           pt_ps[1][:]).then_inc(pt_dve.h, 1)

                def normalise(i, chain, what):
                    sp_, np_ = what
                    wait_apart(dve, rstd_ready, rstd_ready.at(chain.unit, 1))
                    for q in range(QT):
                        chain.step(v_.scalar_tensor_tensor(
                            out=L.c[:, q, :], in0=L.c[:, q, :], scalar=chain.norm.mv[:, q, 0:1],
                            in1=L.rows[:, sp_, 3, :], op0=ALU.subtract, op1=ALU.mult), wait=False)
                    for q in range(QT):
                        chain.wait(1)
                        chain.step(v_.scalar_tensor_tensor(
                            out=L.c[:, q, :], in0=L.c[:, q, :], scalar=chain.norm.rstd[:, q:q + 1],
                            in1=L.rows[:, sp_, 4, :], op0=ALU.mult, op1=ALU.add), wait=False)
                    tiles = [QT * (np_ % GP) + q for q in range(QT)]
                    if sp_ == 0:
                        for q, t in enumerate(tiles):
                            chain.wait(1)
                            chain.step(v_.tensor_scalar(L.h[:, t, :], L.c[:, q, :], 0.0, None, ALU.max),
                                       wait=False, more=BEGUN if q == QT - 1 else 0)
                    else:
                        y_free(i, np_)
                        dve.wait_ge(kept.h, kept.at(graph(i, np_), 1))
                        for q, t in enumerate(tiles):
                            chain.wait(1)
                            chain.step(v_.scalar_tensor_tensor(
                                out=L.y[:, t, :], in0=L.c[:, q, :], scalar=0.0, in1=L.res[:, t, :],
                                op0=ALU.max, op1=ALU.add), wait=False)
                    assert chain.n == (L.sum_steps if sp_ else L.steps)

                def unit(i, u, this, nxt, before, last, early, done):
                    g, gp = stage_unit(i, u), stage_unit(i, u - 1)
                    def begin_unit(u):
                        xT = L.unit_xT[u % 2]
                        for c in range(KC):
                            dve.wait_ge(proj_hi.h, proj_hi.at(stage_unit(i, u), max(c + 1, 2)))
                            low(xT[:, 1, c, :], unit_x(c), xT[:, 0, c, :]
                                ).then_inc(proj_free.h, 1)

                    if this and (done or u == 0):
                        begin_unit(u)
                    if last and not done:
                        normalise(i, Chain(stage_unit(i, u - 2), L.first_steps, 1), last)
                    if this:
                        for q in range(QT):
                            dve.wait_ge(sc_full.h, sc_full.at(g, q + 1))
                            v_.tensor_reduce(L.rowmax[:, q:q + 1], sc_ps[q][:, 0:N], AX.X, ALU.max
                                             ).then_inc(red_done.h, 1)
                            dve.wait_ge(red_done.h, red_done.at(g, q + 1))
                            v_.tensor_scalar(L.negmax[:, q:q + 1], L.rowmax[:, q:q + 1], -L.scale, None,
                                             ALU.mult).then_inc(max_ready.h, 1)
                    if last and last[0] == 1:
                        ending = Chain(stage_unit(i, u - 2), L.sum_steps)
                        ending.statistics([L.y[:, QT * (last[1] % GP) + q, :] for q in range(QT)], LN_EPS)
                        assert ending.n == L.steps
                    if before:
                        hb = QT * ((u - 1) % 2)
                        chain = Chain(gp, norm=1)
                        dve.wait_ge(d_step.h, d_step.at(gp, 3 * QT))
                        dve.wait_ge(hp_ready.h, hp_ready.at(gp, 3 * QT))
                        for q in range(QT):
                            dve.wait_ge(att_full.h, att_full.at(gp, 2 + q))
                            v_.scalar_tensor_tensor(out=L.c[:, q, :], in0=L.hp[:, 1, hb + q, :],
                                                    scalar=L.diag[:, hb + q:hb + q + 1],
                                                    in1=att_ps[(3 * (u - 1) + 1 + q) % 2][:, 0:D],
                                                    op0=ALU.mult, op1=ALU.add).then_inc(att_free.h, 1)
                    if before:
                        for q in range(QT):
                            dve.wait_ge(att_free.h, att_free.at(gp, 2 + q))
                            chain.step(v_.tensor_scalar(L.c[:, q, :], L.c[:, q, :], L.rdel[:, hb + q:hb + q + 1],
                                                        None, ALU.mult), wait=False)
                        chain.statistics([L.c[:, q, :] for q in range(QT)], L2_LN_EPS)
                        assert chain.n == L.first_steps
                    if this:
                        s, n = this
                        if s == 0:
                            dve.wait_ge(adj_loaded[n % GP].h, adj_loaded[n % GP].at(of_parity(i, n), 16))
                        for q in range(QT):
                            t = QT * (u % 2) + q
                            dve.wait_ge(exp_done.h, exp_done.at(g, q + 1))
                            v_.tensor_tensor_reduce(L.delta[:, q, :], L.e[:, q, :], L.adj[:, QT * (n % GP) + q, :],
                                                    1.0, 0.0, ALU.mult, ALU.add, L.dsum[:, q:q + 1]
                                                    ).then_inc(delta_ready.h, 1)
                        for q in range(QT):
                            t = QT * (u % 2) + q
                            dve.wait_ge(delta_ready.h, delta_ready.at(g, q + 1))
                            v_.tensor_tensor_reduce(L.scr[:], L.delta[:, q, P * q:P * q + P], ident[:], 1.0, 0.0,
                                                    ALU.mult, ALU.add, L.diag[:, t:t + 1]).then_inc(d_step.h, 1)
                            v_.scalar_tensor_tensor(out=L.dsum[:, q:q + 1], in0=L.total[:, q:q + 1],
                                                    scalar=L2_SUM_EPS, in1=L.dsum[:, q:q + 1],
                                                    op0=ALU.mult, op1=ALU.add).then_inc(d_step.h, 1)
                            dve.wait_ge(d_step.h, d_step.at(g, 3 * q + 2))
                            v_.reciprocal(L.rdel[:, t:t + 1], L.dsum[:, q:q + 1]).then_inc(d_step.h, 1)
                    if this:
                        dve.wait_ge(att_full.h, att_full.at(g, 1))

                        def block_of(jt, it):
                            return att_ps[3 * u % 2][:, N * jt + P * it:N * jt + P * it + P]
                        v_.tensor_tensor(L.dT[:, 0, :], block_of(0, 0), behind[:], ALU.mult)
                        v_.tensor_tensor(L.dT[:, 2, :], block_of(1, 1), behind[:], ALU.mult)
                        v_.tensor_tensor(L.dT[:, 3, :], block_of(0, 0), ahead[:], ALU.mult)
                        v_.tensor_tensor(L.dT[:, 5, :], block_of(1, 1), ahead[:], ALU.mult)
                        v_.tensor_copy(L.dT[:, 1, :], block_of(1, 0))
                        v_.tensor_copy(L.dT[:, 4, :], block_of(0, 1)).then_inc(att_free.h, 1)
                    if this and nxt and not early:
                        begin_unit(u + 1)
                    if last and last[0] == 1:
                        wait_apart(dve, rstd_ready, rstd_ready.at(stage_unit(i, u - 2), 2))
                        apply(last[1] % GP)
                    if early:
                        normalise(i, chain, before)

                if L.attn:
                    halves(dve, half)
                else:
                    units(dve, unit)
                leave(L)


def kernel(**inputs):
    import numpy as np
    import concourse.bacc as bacc
    from concourse.bass_utils import run_bass_kernel_spmd

    nc = bacc.Bacc("TRN2", target_bir_lowering=False, num_devices=1)
    arrays, aps = {}, {}

    def give(name, a):
        a = np.ascontiguousarray(a)
        arrays[name] = a
        aps[name] = nc.dram_tensor(name, a.shape, mybir.dt.from_np(a.dtype), kind="ExternalInput").ap()

    give("x", np.asarray(inputs["x"]).reshape(B * N, D))
    give("adj", inputs["adj"])
    for name, a in inputs.items():
        a = np.asarray(a)
        if name in ("x", "adj"):
            continue
        if name.startswith("L2_gnn_W"):
            for s in range(2):
                give(f"{name}{s}", a[s].T)
        elif name[:7] in ("L1_gnn_", "L3_gnn_") and name[7] == "W":
            give(name, a.T)
        elif name in ("L0_gnn_bk", "L0_gnn_bq"):
            give(name, a.reshape(J, KC, HD).transpose(0, 2, 1).reshape(P, KC))
        elif a.ndim == 0:
            give(name, a.reshape(1))
        else:
            give(name, a)
    out = nc.dram_tensor("out", (B * N, D), F32, kind="ExternalOutput").ap()
    build(nc, aps["x"], aps["adj"], aps, out)
    r = run_bass_kernel_spmd(nc, [arrays], core_ids=[0])
    return r.results[0]["out"].reshape(B, N, D)
```
